# Optimizing a Trainium2 kernel written in Bass

```python
import numpy as np
import jax
import jax.numpy as jnp

def _softmax(x, axis=-1):
    return jax.nn.softmax(x, axis=axis)

def _gelu(x):
    return jax.nn.gelu(x, approximate=True)

def _silu(x):
    return jax.nn.silu(x)

def _sigmoid(x):
    return jax.nn.sigmoid(x)

def _layernorm(x, axis=-1, eps=1e-05):
    m = jnp.mean(x, axis=axis, keepdims=True)
    v = jnp.var(x, axis=axis, keepdims=True)
    return (x - m) / jnp.sqrt(v + eps)

def _scatter_add(tgt, idx, src, axis=0):
    return tgt.at[idx].add(src)

def _segment_sum(src, seg, n):
    return jax.ops.segment_sum(src, seg, n)
kernel_name = 'mk_gnn_resnorm_d2_gnn_r32_1728c5'

def setup_inputs(seed: int=0):
    np.random.seed(seed)
    _w = jnp.asarray

    def _rec_inputs():
        import jax
        import jax.numpy as jnp
        _gk = jax.random.key(seed)
        x = -0.000202 + 1 * jax.random.normal(jax.random.fold_in(_gk, 1), (3125, 64), jnp.float32)
        _s = jax.random.randint(jax.random.fold_in(_gk, 2), (50000,), 0, 3125, jnp.int32)
        _d = jax.random.randint(jax.random.fold_in(_gk, 3), (50000,), 0, 3125, jnp.int32)
        _loop = jnp.arange(3125, dtype=jnp.int32)
        src = jnp.concatenate([_s, _d, _loop])
        dst = jnp.concatenate([_d, _s, _loop])
        _o = jnp.argsort(dst, stable=True)
        src = src[_o]
        dst = dst[_o]
        edge_attr_32 = -5.16925e-05 + 1.00005 * jax.random.normal(jax.random.fold_in(_gk, 12), (103125, 32), jnp.float32)
        return (x, src, dst, edge_attr_32)
    x, src, dst, edge_attr_32 = _rec_inputs()

    def _L0_gnn_setup():
        import jax, jax.numpy as jnp
        import numpy as np
        N_NODES = 3125
        N_EDGES = 100000
        EDGE_OUT = 32
        HID = 128
        NODE_OUT = 64
        N_GRAPHS = 16
        key = jax.random.key(seed)
        ks = jax.random.split(key, 9)
        x = jax.random.normal(ks[0], (N_NODES, 64), dtype=jnp.float32)
        edge_index = jax.random.randint(ks[1], (2, N_EDGES), 0, N_NODES, dtype=jnp.int64)
        edge_attr = jax.random.normal(ks[2], (N_EDGES, EDGE_OUT), dtype=jnp.float32)
        u = jax.random.normal(ks[3], (N_GRAPHS, 1), dtype=jnp.float32)
        batch = jnp.sort(jax.random.randint(ks[4], (N_NODES,), 0, N_GRAPHS, dtype=jnp.int64))
        d_in = 3 * EDGE_OUT + 1
        W1 = jax.random.normal(ks[5], (d_in, HID), dtype=jnp.float32) / np.sqrt(d_in)
        b1 = jnp.zeros((HID,), dtype=jnp.float32)
        W2 = jax.random.normal(ks[6], (HID, NODE_OUT), dtype=jnp.float32) / np.sqrt(HID)
        b2 = jnp.zeros((NODE_OUT,), dtype=jnp.float32)
        return {'x': x, 'edge_index': edge_index, 'edge_attr': edge_attr, 'u': u, 'batch': batch, 'W1': W1, 'b1': b1, 'W2': W2, 'b2': b2}
    _L0_gnn_all = _L0_gnn_setup()
    _L0_gnn_in = {k: v for k, v in _L0_gnn_all.items() if k in ('u', 'W1', 'b1', 'W2', 'b2')}
    del _L0_gnn_all

    def _L1_gnn_setup():
        import jax, jax.numpy as jnp
        import numpy as np
        N_NODES = 50000
        N_EDGES = 50000
        C = 64
        EDGE_H = 64
        RAW_EDGE = 32
        NUM_LAYERS = 3
        NEG_SLOPE = 0.2

        def _gatv2_layer(x, src, dst, e_proj, Wl, bl, Wr, br, att, bias, n_nodes):
            xl = x @ Wl + bl
            xr = x @ Wr + br
            e = xl[src] + xr[dst] + e_proj
            e = jnp.where(e > 0, e, NEG_SLOPE * e)
            s = e @ att
            m = jax.ops.segment_max(s, dst, num_segments=n_nodes)
            m = jnp.where(jnp.isfinite(m), m, 0.0)
            a = jnp.exp(s - m[dst])
            denom = jax.ops.segment_sum(a, dst, num_segments=n_nodes)
            alpha = a / (denom[dst] + 1e-16)
            out = jax.ops.segment_sum(xl[src] * alpha[:, None], dst, num_segments=n_nodes)
            return out + bias
        key = jax.random.key(seed)
        ks = jax.random.split(key, 16)
        inp = {'x': jax.random.normal(ks[0], (N_NODES, C), dtype=jnp.float32), 'edge_index': jax.random.randint(ks[1], (2, N_EDGES), 0, N_NODES, dtype=jnp.int64), 'edge_attr': jax.random.normal(ks[2], (N_EDGES, RAW_EDGE), dtype=jnp.float32), 'W_emb': jax.random.normal(ks[3], (RAW_EDGE, EDGE_H), dtype=jnp.float32) * RAW_EDGE ** (-0.5), 'b_emb': jnp.zeros((EDGE_H,), dtype=jnp.float32), 'Wl': jax.random.normal(ks[4], (NUM_LAYERS, C, C), dtype=jnp.float32) * C ** (-0.5), 'bl': jnp.zeros((NUM_LAYERS, C), dtype=jnp.float32), 'Wr': jax.random.normal(ks[5], (NUM_LAYERS, C, C), dtype=jnp.float32) * C ** (-0.5), 'br': jnp.zeros((NUM_LAYERS, C), dtype=jnp.float32), 'We': jax.random.normal(ks[6], (NUM_LAYERS, EDGE_H, C), dtype=jnp.float32) * EDGE_H ** (-0.5), 'att': jax.random.normal(ks[7], (NUM_LAYERS, C), dtype=jnp.float32) * C ** (-0.5), 'bias': jnp.zeros((NUM_LAYERS, C), dtype=jnp.float32)}
        return inp
    _L1_gnn_all = _L1_gnn_setup()
    _L1_gnn_in = {k: v for k, v in _L1_gnn_all.items() if k in ('W_emb', 'b_emb', 'Wl', 'bl', 'Wr', 'br', 'We', 'att', 'bias')}
    del _L1_gnn_all
    return {'x': x, 'src': src, 'dst': dst, 'edge_attr_32': edge_attr_32, 'L0_gnn_u': _L0_gnn_in['u'], 'L0_gnn_W1': _L0_gnn_in['W1'], 'L0_gnn_b1': _L0_gnn_in['b1'], 'L0_gnn_W2': _L0_gnn_in['W2'], 'L0_gnn_b2': _L0_gnn_in['b2'], 'L1_gnn_W_emb': _L1_gnn_in['W_emb'], 'L1_gnn_b_emb': _L1_gnn_in['b_emb'], 'L1_gnn_Wl': _L1_gnn_in['Wl'], 'L1_gnn_bl': _L1_gnn_in['bl'], 'L1_gnn_Wr': _L1_gnn_in['Wr'], 'L1_gnn_br': _L1_gnn_in['br'], 'L1_gnn_We': _L1_gnn_in['We'], 'L1_gnn_att': _L1_gnn_in['att'], 'L1_gnn_bias': _L1_gnn_in['bias']}

def reference(x, src, dst, edge_attr_32, L0_gnn_u, L0_gnn_W1, L0_gnn_b1, L0_gnn_W2, L0_gnn_b2, L1_gnn_W_emb, L1_gnn_b_emb, L1_gnn_Wl, L1_gnn_bl, L1_gnn_Wr, L1_gnn_br, L1_gnn_We, L1_gnn_att, L1_gnn_bias):
    import jax
    import jax.numpy as jnp

    def _L0_gnn_ref(x, edge_index, edge_attr, u, batch, W1, b1, W2, b2):
        import jax, jax.numpy as jnp
        import numpy as np
        N_NODES = 3125
        N_EDGES = 100000
        EDGE_OUT = 32
        HID = 128
        NODE_OUT = 64
        N_GRAPHS = 16
        N = x.shape[0]
        row = edge_index[0]
        seg_sum = jax.ops.segment_sum(edge_attr, row, num_segments=N)
        seg_max = jax.ops.segment_max(edge_attr, row, num_segments=N)
        cnt = jax.ops.segment_sum(jnp.ones((edge_attr.shape[0], 1), edge_attr.dtype), row, num_segments=N)
        seg_mean = seg_sum / jnp.maximum(cnt, 1.0)
        seg_max = jnp.where(cnt > 0, seg_max, 0.0)
        h = jnp.concatenate([seg_sum, seg_max, seg_mean, u[batch]], axis=1)
        h = jax.nn.relu(h @ W1 + b1)
        return h @ W2 + b2

    def _L1_gnn_ref(x, edge_index, edge_attr, W_emb, b_emb, Wl, bl, Wr, br, We, att, bias):
        import jax, jax.numpy as jnp
        import numpy as np
        N_NODES = 50000
        N_EDGES = 50000
        C = 64
        EDGE_H = 64
        RAW_EDGE = 32
        NUM_LAYERS = 3
        NEG_SLOPE = 0.2

        def _gatv2_layer(x, src, dst, e_proj, Wl, bl, Wr, br, att, bias, n_nodes):
            xl = x @ Wl + bl
            xr = x @ Wr + br
            e = xl[src] + xr[dst] + e_proj
            e = jnp.where(e > 0, e, NEG_SLOPE * e)
            s = e @ att
            m = jax.ops.segment_max(s, dst, num_segments=n_nodes)
            m = jnp.where(jnp.isfinite(m), m, 0.0)
            a = jnp.exp(s - m[dst])
            denom = jax.ops.segment_sum(a, dst, num_segments=n_nodes)
            alpha = a / (denom[dst] + 1e-16)
            out = jax.ops.segment_sum(xl[src] * alpha[:, None], dst, num_segments=n_nodes)
            return out + bias
        n = x.shape[0]
        edge_h = edge_attr @ W_emb + b_emb
        loop = jnp.arange(n, dtype=edge_index.dtype)
        src = jnp.concatenate([edge_index[0], loop])
        dst = jnp.concatenate([edge_index[1], loop])
        mean_eh = jnp.mean(edge_h, axis=0)
        edge_h_full = jnp.concatenate([edge_h, jnp.broadcast_to(mean_eh, (n, EDGE_H))], axis=0)
        h = x
        for l in range(NUM_LAYERS):
            e_proj = edge_h_full @ We[l]
            h = _gatv2_layer(h, src, dst, e_proj, Wl[l], bl[l], Wr[l], br[l], att[l], bias[l], n)
            if l < NUM_LAYERS - 1:
                h = jax.nn.relu(h)
        return h
    edge_index = jnp.stack([src, dst])
    batch0 = jnp.zeros((3125,), jnp.int32)
    x = _layernorm(x + _L0_gnn_ref(x, edge_index, edge_attr_32, L0_gnn_u, batch0, L0_gnn_W1, L0_gnn_b1, L0_gnn_W2, L0_gnn_b2), axis=-1)
    x = _layernorm(x + _L1_gnn_ref(x, edge_index, edge_attr_32, L1_gnn_W_emb, L1_gnn_b_emb, L1_gnn_Wl, L1_gnn_bl, L1_gnn_Wr, L1_gnn_br, L1_gnn_We, L1_gnn_att, L1_gnn_bias), axis=-1)
    return x

_drawn_inputs = setup_inputs


def setup_inputs(seed=0):
    import zlib

    import numpy as np

    out = dict(_drawn_inputs(seed))
    spreads = {'L0_gnn_b1': (0.0, 0.289),
     'L0_gnn_b2': (0.0, 0.1),
     'L1_gnn_b_emb': (0.0, 0.8),
     'L1_gnn_bl': (0.0, 0.1),
     'L1_gnn_br': (0.0, 2.0),
     'L1_gnn_bias': (0.0, 0.1)}
    factors = {'L0_gnn_u': 3.019, 'L1_gnn_W_emb': 8.0, 'L1_gnn_Wr': 8.0, 'L1_gnn_We': 8.0}
    for name, (base, spread) in spreads.items():
        noise = np.random.default_rng([zlib.crc32(name.encode()), seed]).standard_normal(out[name].shape)
        drawn = base * np.exp(spread * noise) if base else spread * noise
        out[name] = jnp.asarray(drawn.astype(out[name].dtype))
    for name, factor in factors.items():
        out[name] = (out[name] * factor).astype(out[name].dtype)
    return out
```

```python
from contextlib import ExitStack

import concourse.bass as bass
import concourse.mybir as mybir

F32, BF16, I32, U32 = mybir.dt.float32, mybir.dt.bfloat16, mybir.dt.int32, mybir.dt.uint32
ALU, ACT, AX = mybir.AluOpType, mybir.ActivationFunctionType, mybir.AxisListType
ENG = mybir.EngineType

P = 128
NODES, EDGES = 3125, 103125
EC, C, HID, LAYERS = 32, 64, 128, 3
G = 24
NG = 34
T = G * NG
ROWS = T * P
NT = 25
NPAD = NT * P
ACCW = NPAD + P
LO = 64
HI = NPAD // LO
HL = HI + LO
RW = EC + 1
QUARTERS = 4
STEPS = T // QUARTERS // 4
QROWS = ROWS // QUARTERS
BAT = 8
SC = C + 2
BIG = 1e30
NEG_SLOPE, EPS, DEN_EPS = 0.2, 1e-5, 1e-16
WIN = "node ids lie in [0, 3125]"


class Named:
    pass


def b3(ap, n):
    return ap[:, :, None].to_broadcast([ap.shape[0], ap.shape[1], n])


def rep(ap, n):
    return ap[:, None, :].to_broadcast([ap.shape[0], n, ap.shape[1]])


def alone(eng, k):
    eng.sem_inc(k.passed, 1)


def chain(eng, sem):
    count = [0]

    def run(ins):
        count[0] += 1
        ins.then_inc(sem, 1)
        eng.wait_ge(sem, count[0])
    return run


def setup(nc, k, d):
    with ExitStack() as c:
        def sb(name, shape, dt=F32):
            return c.enter_context(nc.sbuf_tensor(name, shape, dt))

        def sem(name):
            return c.enter_context(nc.semaphore(name))
        iota_i = sb("iota_i", [P, P], I32)
        hi_i, lo_i = sb("hi_i", [P, T], I32), sb("lo_i", [P, T], I32)
        dst_i = sb("dst_i", [P, T], I32)
        dstg_i = sb("dstg_i", [G, NG * P], I32)
        last_i = sb("last_i", [1, T], I32)
        last_f, single = sb("last_f", [1, T]), sb("single", [1, T])
        dst_f = sb("dst_f", [P, T])
        emb4, embx = sb("emb4", [C, P]), sb("embx", [C, C + 1])
        we = sb("we", [C, LAYERS, C])
        ids_in, weights_in = sem("ids_in"), sem("weights_in")
        pool_step, dve_step, const_ready = sem("setup_pool"), sem("setup_dve"), sem("const_ready")
        dstf_ready, base_ready, emb_ready, wc_ready = sem("dstf_ready"), sem("base_ready"), sem("emb_ready"), sem("wc_ready")
        zero_ready, zero_out = sem("zero_ready"), sem("zero_out")
        base_ps = [c.enter_context(nc.psum_tensor(f"base_ps{h}", [P, 512], F32)) for h in range(2)]
        wc_ps = c.enter_context(nc.psum_tensor("wc_ps", [P, 512], F32))
        wx_ps = c.enter_context(nc.psum_tensor("wx_ps", [P, 512], F32))
        block = c.enter_context(nc.Block())

        @block.sync
        def _(sp):
            sp.dma_start(k.src_i[:], d.src).then_inc(ids_in, 16)
            sp.dma_start(dst_i[:], d.dst).then_inc(ids_in, 16)
            sp.dma_start(dstg_i[:], d.dstg).then_inc(ids_in, 16)
            sp.dma_start(last_i[:], d.dst[P - 1:P, :]).then_inc(ids_in, 16)
            sp.dma_start(k.base_i[:], d.dst[0:1, :]).then_inc(ids_in, 16)
            sp.dma_start(k.x[:], d.x).then_inc(weights_in, 16)
            sp.dma_start(k.w1[0:97, :], d.w1).then_inc(weights_in, 16)
            sp.dma_start(k.w1[97:98, :], d.b1[None, :]).then_inc(weights_in, 16)
            sp.dma_start(k.w2[:], d.w2).then_inc(weights_in, 16)
            sp.dma_start(k.b2[:], d.b2.partition_broadcast(P)).then_inc(weights_in, 16)
            sp.dma_start(k.u[:], d.u[0].partition_broadcast(P)).then_inc(weights_in, 16)
            sp.dma_start(k.att_all[:], d.att.partition_broadcast(P)).then_inc(weights_in, 16)
            sp.dma_start(k.bias_all[:], d.bias.partition_broadcast(P)).then_inc(weights_in, 16)
            sp.dma_start(k.wlr_all[0:C, :, 0:C], d.wl.rearrange("l c n -> c l n")).then_inc(weights_in, 16)
            sp.dma_start(k.wlr_all[0:C, :, C:2 * C], d.wr.rearrange("l c n -> c l n")).then_inc(weights_in, 16)
            sp.dma_start(k.wlr_all[C:C + 1, :, 0:C], d.bl[None]).then_inc(weights_in, 16)
            sp.dma_start(k.wlr_all[C:C + 1, :, C:2 * C], d.br[None]).then_inc(weights_in, 16)
            sp.dma_start(we[:], d.we.rearrange("l c n -> c l n")).then_inc(weights_in, 16)
            sp.wait_ge(zero_ready, 1)
            for q in range(QUARTERS):
                sp.dma_start(emb4[:, EC * q:EC * (q + 1)], d.wembt).then_inc(weights_in, 16)
            sp.dma_start(embx[:, C:C + 1], d.bemb).then_inc(weights_in, 16)
            sp.wait_ge(zero_ready, 2)
            sp.dma_start(d.xr_d[NPAD:NPAD + P, :], k.acc[:, 0:C]).then_inc(zero_out, 16)
            sp.wait_ge(zero_out, 16)

        @block.gpsimd
        def _(pool):
            pool.iota(iota_i[:], [[1, P]], base=0, channel_multiplier=0).then_inc(const_ready, 1)
            pool.memset(embx[:], 0.0).then_inc(zero_ready, 1)
            pool.memset(k.acc[:], 0.0).then_inc(zero_ready, 1)
            pool.memset(k.ident[:], 0.0).then_inc(pool_step, 1)
            pool.memset(k.earlier[:], 1.0).then_inc(pool_step, 1)
            pool.memset(k.upper[:], 1.0).then_inc(pool_step, 1)
            pool.memset(k.spread[:], 1.0).then_inc(pool_step, 1)
            pool.memset(k.sum_rows[:], 0.0).then_inc(pool_step, 1)
            pool.wait_ge(pool_step, 5)
            pool.affine_select(out=k.ident[:], in_=k.ident[:], compare_op=ALU.not_equal, fill=1.0, base=0,
                               pattern=[[-1, P]], channel_multiplier=1).then_inc(const_ready, 1)
            pool.affine_select(out=k.earlier[:], in_=k.earlier[:], compare_op=ALU.is_gt, fill=0.0, base=0,
                               pattern=[[-1, P]], channel_multiplier=1).then_inc(const_ready, 1)
            pool.affine_select(out=k.upper[:], in_=k.upper[:], compare_op=ALU.is_gt, fill=0.0, base=0,
                               pattern=[[1, HI]], channel_multiplier=-1).then_inc(const_ready, 1)
            pool.affine_select(out=k.spread[:], in_=k.spread[:], compare_op=ALU.is_ge, fill=0.0, base=0,
                               pattern=[[1, P]], channel_multiplier=-EC).then_inc(pool_step, 1)
            pool.wait_ge(pool_step, 6)
            pool.affine_select(out=k.spread[:], in_=k.spread[:], compare_op=ALU.is_ge, fill=0.0, base=EC - 1,
                               pattern=[[-1, P]], channel_multiplier=EC).then_inc(const_ready, 1)
            pool.memset(k.ones[:], 1.0).then_inc(const_ready, 1)
            pool.memset(k.sum_rows[:, 0:SC - 1], 1.0).then_inc(const_ready, 1)
            pool.memset(k.hT[:], 1.0).then_inc(const_ready, 1)
            pool.memset(k.bd_all[:], 0.0).then_inc(const_ready, 1)

        @block.vector
        def _(dve):
            step = chain(dve, dve_step)
            dve.wait_ge(ids_in, 80)
            dve.tensor_copy(dst_f[:], dst_i[:]).then_inc(dstf_ready, 1)
            dve.tensor_copy(k.dstg[:], dstg_i[:])
            dve.tensor_copy(last_f[:], last_i[:])
            dve.tensor_scalar(hi_i[:], k.src_i[:], 6, None, ALU.logical_shift_right)
            step(dve.tensor_scalar(lo_i[:], k.src_i[:], LO - 1, None, ALU.bitwise_and))
            dve.tensor_copy(k.hi[:], hi_i[:])
            dve.tensor_copy(k.lo[:], lo_i[:])
            step(dve.memset(k.cont_b[:], 0.0))
            dve.tensor_tensor(k.cont_b[:, 1:T], dst_f[0:1, 1:T], last_f[:, 0:T - 1], ALU.is_equal)
            step(dve.tensor_tensor(single[:], dst_f[0:1, :], last_f[:], ALU.is_equal))
            step(dve.tensor_tensor(k.carry_b[:], k.cont_b[:], single[:], ALU.mult))
            dve.tensor_scalar(k.cont_b[:], k.cont_b[:], -1.0, BIG, ALU.add, ALU.mult)
            dve.tensor_scalar(k.carry_b[:], k.carry_b[:], -1.0, BIG, ALU.add, ALU.mult)
            dve.memset(k.carry[:], -BIG)
            dve.memset(k.eq[:], 0.0)
            dve.memset(k.one[:], 1.0)
            dve.wait_ge(const_ready, 9)
            step(dve.tensor_copy(k.iota[:], iota_i[:]))
            step(dve.tensor_copy(k.iota_b[:], k.iota[:, 0:LO]))
            dve.wait_ge(base_ready, 1)
            for h in range(2):
                dve.tensor_tensor(k.loc[:, h * T // 2:(h + 1) * T // 2], dst_f[:, h * T // 2:(h + 1) * T // 2],
                                  base_ps[h][:, 0:T // 2], ALU.subtract)
            dve.wait_ge(wc_ready, 1)
            dve.tensor_copy(k.wc[:], wc_ps[0:EC, 0:LAYERS * C])
            for q in range(QUARTERS):
                s = slice(EC * q, EC * (q + 1))
                dve.tensor_copy(k.bd_all[s, :, q * C:(q + 1) * C],
                                wc_ps[s, 0:LAYERS * C].rearrange("p (l n) -> p l n", l=LAYERS))
            brow = k.wlr_all[C:C + 1, :, C:2 * C]
            step(dve.tensor_tensor(brow, brow, wx_ps[C:C + 1, 0:LAYERS * C].rearrange("p (l n) -> p l n", l=LAYERS),
                                   ALU.add))
            dve.memset(k.floor[:], 0.0).then_inc(emb_ready, 1)
            dve.wait_ge(emb_ready, 1)
            step(dve.memset(k.floor[:, LAYERS - 1:LAYERS], -BIG))

        @block.tensor
        def _(pe):
            pe.wait_ge(dstf_ready, 1)
            pe.wait_ge(const_ready, 9)
            for h in range(2):
                mm = pe.matmul(base_ps[h][:, 0:T // 2], k.ones[0:1, 0:P], dst_f[0:1, h * T // 2:(h + 1) * T // 2],
                               start=True, stop=True)
            mm.then_inc(base_ready, 1)
            pe.wait_ge(weights_in, 16 * 18)
            pe.matmul(wc_ps[:, 0:LAYERS * C], emb4[:], we[:].rearrange("p l n -> p (l n)"), start=True, stop=True)
            pe.matmul(wx_ps[0:C + 1, 0:LAYERS * C], embx[:], we[:].rearrange("p l n -> p (l n)"),
                      start=True, stop=True).then_inc(wc_ready, 1)


def one_hots(nc, dve, k, oh, t0):
    dve.tensor_tensor(oh[:, :, 0:HI], rep(k.iota_b[:, 0:HI], G), b3(k.hi[:, bass.ds(t0, G)], HI), ALU.is_equal)
    return dve.tensor_tensor(oh[:, :, HI:HL], rep(k.iota_b[:], G), b3(k.lo[:, bass.ds(t0, G)], LO), ALU.is_equal)


def histogram(nc, k, d):
    with ExitStack() as c:
        def sb(name, shape, dt=F32):
            return c.enter_context(nc.sbuf_tensor(name, shape, dt))

        def sem(name):
            return c.enter_context(nc.semaphore(name))
        oh = [sb(f"oh_h{u}", [P, G, HL], BF16) for u in range(2)]
        counts, upto, rows_of = sb("counts", [HI, LO]), sb("upto", [HI, LO]), sb("node_rows", [NT, 2, P])
        oh_ready, oh_used, counted = sem("oh_ready"), sem("oh_used"), sem("counted")
        upto_ready, off_ready, dve_step, table_ready = sem("upto_ready"), sem("off_ready"), sem("hist_dve"), sem("table_ready")
        table_out, table_in, turned = sem("table_out"), sem("table_in"), sem("turned")
        cps = c.enter_context(nc.psum_tensor("counts_ps", [P, 512], F32))
        ops = c.enter_context(nc.psum_tensor("offset_ps", [P, 512], F32))
        block = c.enter_context(nc.Block())

        @block.vector
        def _(dve):
            with dve.Fori(0, NG // 2) as i:
                for u in range(2):
                    dve.wait_ge(oh_used, 2 * i + u + 1)
                    one_hots(nc, dve, k, oh[u], (2 * i + u) * G).then_inc(oh_ready, 1)
            step = chain(dve, dve_step)
            dve.wait_ge(counted, 1)
            step(dve.tensor_copy(counts[:], cps[0:HI, 0:LO]))
            dve.tensor_tensor_scan(upto[:], k.ones[0:HI, 0:LO], counts[:], 0.0, ALU.mult, ALU.add).then_inc(upto_ready, 1)
            dve.wait_ge(upto_ready, 1)
            dve.wait_ge(off_ready, 1)
            step(dve.tensor_tensor(upto[:], upto[:], counts[:], ALU.subtract))
            dve.tensor_scalar(k.count_ring[0][:, 0, :], upto[:], ops[0:HI, 0:1], None, ALU.add).then_inc(table_ready, 1)
            dve.wait_ge(turned, 1)
            dve.tensor_copy(k.start_n[:], ops[:, 64:64 + NT])
            dve.tensor_copy(k.count_n[:], ops[:, 128:128 + NT])

        @block.tensor
        def _(pe):
            pe.matmul(cps[0:HI, 0:LO], k.sum_rows[0:1, SC - 1:SC].to_broadcast([1, HI]),
                      k.ones[0:1, 0:LO], start=True, stop=False, skip_group_check=True)
            pe.sem_inc(oh_used, 2)
            with pe.Fori(0, NG // 2) as i:
                for u in range(2):
                    pe.wait_ge(oh_ready, 2 * i + u + 1)
                    for j in range(G):
                        mm = pe.matmul(cps[0:HI, 0:LO], oh[u][:, j, 0:HI], oh[u][:, j, HI:HL],
                                       start=False, stop=False, skip_group_check=True)
                    mm.then_inc(oh_used, 1)
            pe.wait_ge(oh_used, NG + 2)
            pe.matmul(cps[0:HI, 0:LO], k.sum_rows[0:1, SC - 1:SC].to_broadcast([1, HI]),
                      k.ones[0:1, 0:LO], start=False, stop=True, skip_group_check=True).then_inc(counted, 1)
            pe.wait_ge(upto_ready, 1)
            pe.matmul(ops[0:HI, 0:1], k.upper[:], upto[:, LO - 1:LO], start=True, stop=True).then_inc(off_ready, 1)
            pe.wait_ge(table_in, 32)
            pe.wait_ge(table_ready, 1)
            pe.transpose(ops[:, 64:64 + NT], rows_of[:, 0, :], k.ident[0:NT, 0:NT])
            pe.transpose(ops[:, 128:128 + NT], rows_of[:, 1, :], k.ident[0:NT, 0:NT]).then_inc(turned, 1)

        @block.sync
        def _(sp):
            sp.wait_ge(table_ready, 1)
            sp.dma_start(d.tables[0].rearrange("(h l) -> h l", l=LO), k.count_ring[0][:, 0, :]).then_inc(table_out, 16)
            sp.dma_start(d.tables[1].rearrange("(h l) -> h l", l=LO), counts[:]).then_inc(table_out, 16)
            sp.wait_ge(table_out, 32)
            for m in range(2):
                sp.dma_start(rows_of[:, m, :], d.tables[m].rearrange("(i p) -> i p", p=P)).then_inc(table_in, 16)


def sort(nc, k, d):
    with ExitStack() as c:
        def sb(name, shape, dt=F32):
            return c.enter_context(nc.sbuf_tensor(name, shape, dt))

        def ps(name, dt=F32, n=512):
            return c.enter_context(nc.psum_tensor(name, [P, n], dt))

        def sem(name):
            return c.enter_context(nc.semaphore(name))
        oh = [sb(f"oh_s{u}", [P, G, HL], BF16) for u in range(2)]
        rows = [sb(f"rows{u}", [P, G, RW]) for u in range(2)]
        place = [sb(f"place{u}", [P, G], I32) for u in range(2)]
        hi_t = sb("hi_t", [HI, BAT, P])
        same, picked = sb("same", [P, BAT, P]), sb("picked", [P, BAT, LO])
        rank, before = sb("rank", [P, BAT]), sb("before", [P, BAT])
        ident_b = sb("ident_b", [P, P], BF16)
        hp = ps("hi_ps", BF16, BAT * P)
        dp, lp = ps("delta_ps"), ps("lookup_ps")
        bp = [ps(f"source_ps{n}") for n in range(2)]
        rows_in = [sem(f"rows_in{u}") for u in range(2)]
        scattered = [sem(f"scattered{u}") for u in range(2)]
        oh_ready, src_ready, place_ready, ident_ready = sem("s_oh_ready"), sem("src_ready"), sem("place_ready"), sem("ident_ready")
        hi_turned, hi_ready, delta_ready, ring_ready = sem("hi_turned"), sem("hi_ready"), sem("delta_ready"), sem("ring_ready")
        source_ready, source_used, found, found_used = sem("source_ready"), sem("source_used"), sem("found"), sem("found_used")
        picked_ready, before_ready, rows_free = sem("picked_ready"), sem("before_ready"), sem("rows_free")
        block = c.enter_context(nc.Block())
        B3 = G // BAT

        @block.sync
        def _(sp):
            with sp.Fori(0, NG // 2) as i:
                for u in range(2):
                    g = 2 * i + u
                    sp.wait_ge(rows_free, g + 1)
                    sp.dma_start(rows[u][:, :, 0:EC], d.attr[:, bass.ds(g * G, G), :]).then_inc(rows_in[u], 16)

        @block.gpsimd
        def _(pool):
            pool.sem_inc(rows_free, 2)

            def both(i, first):
                for u in range(2):
                    pool.wait_ge(place_ready, 2 * i + u + 1)
                    pool.wait_ge(rows_in[u], 16 * (i + 1))
                    alone(pool, k)
                    for j in range(G):
                        if j == BAT and not (first and u == 0):
                            pool.wait_ge(scattered[1 - u], 16 * G * (i + u))
                            pool.sem_inc(rows_free, 1)
                        pool.indirect_dma_start(
                            d.sorted, bass.IndirectOffsetOnAxis(place[u][:, j:j + 1].bitcast(U32), 0),
                            rows[u][:, j, :], None).then_inc(scattered[u], 16)

            both(0, True)
            with pool.Fori(1, NG // 2) as i:
                both(i, False)
            pool.wait_ge(scattered[1], 16 * G * (NG // 2))

        @block.vector
        def _(dve):
            dve.tensor_copy(ident_b[:], k.ident[:]).then_inc(ident_ready, 1)
            with dve.Fori(0, NG // 2) as i:
                for u in range(2):
                    g = 2 * i + u
                    one_hots(nc, dve, k, oh[u], g * G).then_inc(oh_ready, 1)
                    dve.wait_ge(rows_free, g + 1)
                    dve.scalar_tensor_tensor(rows[u][:, :, EC], k.hi[:, bass.ds(g * G, G)], float(LO),
                                             k.lo[:, bass.ds(g * G, G)], ALU.mult, ALU.add).then_inc(src_ready, 1)
                    for q in range(B3):
                        b = B3 * g + q
                        dve.wait_ge(delta_ready, b + 1)
                        for j in range(BAT):
                            t = q * BAT + j
                            now = k.count_ring[u][:, t, :]
                            after = k.count_ring[u][:, t + 1, :] if t + 1 < G else k.count_ring[1 - u][:, 0, :]
                            if j:
                                dve.wait_ge(ring_ready, BAT * b + j)
                            dve.tensor_tensor(after, now, dp[0:HI, j * LO:(j + 1) * LO], ALU.add).then_inc(ring_ready, 1)
                        for j in range(BAT):
                            if j % 4 == 0:
                                dve.wait_ge(source_ready, 2 * b + j // 4 + 1)
                            ins = dve.scalar_tensor_tensor(
                                same[:, j, :], bp[j // 4][:, (j % 4) * P:(j % 4 + 1) * P],
                                rows[u][:, q * BAT + j, EC:EC + 1], k.earlier[:], ALU.is_equal, ALU.mult,
                                accum_out=rank[:, j:j + 1])
                            if j % 4 == 3:
                                ins.then_inc(source_used, 1)
                        dve.wait_ge(found, b + 2)
                        dve.tensor_tensor(picked[:], lp[:].rearrange("p (j n) -> p j n", n=LO),
                                          oh[u][:, q * BAT:(q + 1) * BAT, HI:HL], ALU.mult).then_inc(picked_ready, 1)
                        dve.wait_ge(picked_ready, b + 1)
                        dve.tensor_reduce(before[:], picked[:], AX.X, ALU.add).then_inc(before_ready, 1)
                        dve.wait_ge(before_ready, b + 1)
                        dve.wait_ge(source_used, 2 * b + 2 + 2)
                        ins = dve.tensor_tensor(place[u][:, q * BAT:(q + 1) * BAT], before[:], rank[:], ALU.add)
                        if q == B3 - 1:
                            ins.then_inc(place_ready, 1)

        @block.scalar
        def _(act):
            act.sem_inc(found, 1)
            with act.Fori(0, NG * B3) as b:
                act.wait_ge(hi_turned, b + 1)
                act.wait_ge(found, b + 1)
                act.activation(hi_t[:], hp[0:HI, :].rearrange("p (j n) -> p j n", n=P), ACT.Copy).then_inc(hi_ready, 1)

        @block.tensor
        def _(pe):
            pe.wait_ge(ident_ready, 1)
            pe.sem_inc(source_used, 2)
            with pe.Fori(0, NG // 2) as i:
                for u in range(2):
                    g = 2 * i + u
                    pe.wait_ge(oh_ready, g + 1)
                    pe.wait_ge(src_ready, g + 1)
                    alone(pe, k)
                    for q in range(B3):
                        b = B3 * g + q
                        for j in range(BAT):
                            mm = pe.transpose(hp[0:HI, j * P:(j + 1) * P], oh[u][:, q * BAT + j, 0:HI], ident_b[:])
                        mm.then_inc(hi_turned, 1)
                        for j in range(BAT):
                            mm = pe.matmul(dp[0:HI, j * LO:(j + 1) * LO], oh[u][:, q * BAT + j, 0:HI],
                                           oh[u][:, q * BAT + j, HI:HL], start=True, stop=True, skip_group_check=True)
                        mm.then_inc(delta_ready, 1)
                        for j in range(BAT):
                            if j % 4 == 0:
                                pe.wait_ge(source_used, 2 * b + j // 4 + 1)
                            mm = pe.matmul(bp[j // 4][:, (j % 4) * P:(j % 4 + 1) * P],
                                           rows[u][:, q * BAT + j, EC:EC + 1].to_broadcast([P, P]), k.ident[:],
                                           start=True, stop=True, skip_group_check=True)
                            if j % 4 == 3:
                                mm.then_inc(source_ready, 1)
                        pe.wait_ge(hi_ready, b + 1)
                        pe.wait_ge(ring_ready, BAT * (b + 1))
                        for j in range(BAT):
                            mm = pe.matmul(lp[:, j * LO:(j + 1) * LO], hi_t[:, j, :], k.count_ring[u][:, q * BAT + j, :],
                                           start=True, stop=True, skip_group_check=True)
                        mm.then_inc(found, 1)


def scan(nc, k, d):
    R = 3
    W = 4 * P
    with ExitStack() as c:
        def sb(name, shape, dt=F32):
            return c.enter_context(nc.sbuf_tensor(name, shape, dt))

        def ps(name):
            return c.enter_context(nc.psum_tensor(name, [P, W], F32))

        def sem(name):
            return c.enter_context(nc.semaphore(name))
        rin = [sb(f"rin{r}", [P, QUARTERS, 4 * RW]) for r in range(R)]
        attr = [sb(f"attr{r}", [P, 4, QUARTERS * EC]) for r in range(R)]
        srow = sb("srow", [QUARTERS, W])
        ids = [sb(f"ids{r}", [P, W + 1]) for r in range(R)]
        same, bar = sb("same_src", [P, W]), sb("bar", [P, W])
        mx = [sb(f"mx{r}", [P, W]) for r in range(R)]
        sm = [sb(f"sm{r}", [P, W]) for r in range(R)]
        rout = [sb(f"rout{r}", [P, QUARTERS, 4, 2 * EC]) for r in range(R)]
        attr_ps = [ps(f"attr_ps{r}") for r in range(R)]
        srow_ps, ids_ps, mback, sback = ps("srow_ps"), ps("ids_ps"), ps("mback"), ps("sback")
        loaded = [sem(f"loaded{r}") for r in range(R)]
        stored = [sem(f"stored{r}") for r in range(R)]
        attr_copied, src_turned, src_copied = sem("attr_copied"), sem("src_turned"), sem("src_copied")
        ids_spread, ids_ready, attr_turned = sem("ids_spread"), sem("ids_ready"), sem("attr_turned")
        edge_ready, scanned, back_ready, back_copied, init, flags = (
            sem("ids_first"), sem("scanned"), sem("back_ready"), sem("back_copied"), sem("scan_init"), sem("flags"))
        src_v = d.sorted.rearrange("(g s p k) c -> p s g (k c)", g=QUARTERS, s=STEPS, p=P)
        out_v = d.runs.rearrange("(g s p k) c -> p s g (k c)", g=QUARTERS, s=STEPS, p=P)
        block = c.enter_context(nc.Block())

        @block.sync
        def _(sp):
            with sp.Fori(0, STEPS // R) as i:
                for r in range(R):
                    n = R * i + r
                    sp.wait_ge(attr_copied, n + 1)
                    sp.wait_ge(src_turned, n + 1)
                    sp.dma_start(rin[r][:, None], src_v[:, bass.ds(n, 1)]).then_inc(loaded[r], 16)

        @block.gpsimd
        def _(pool):
            pool.sem_inc(attr_copied, R)
            with pool.Fori(0, STEPS // R) as i:
                for r in range(R):
                    pool.wait_ge(attr_turned, R * i + r + 1)
                    pool.wait_ge(loaded[r], 16 * (i + 1))
                    alone(pool, k)
                    pool.tensor_copy(attr[r][:].rearrange("p k (g c) -> p g k c", c=EC),
                                     rin[r][:].rearrange("p g (k c) -> p g k c", c=RW)[:, :, :, 0:EC])\
                        .then_inc(attr_copied, 1)

        @block.tensor
        def _(pe):
            pe.sem_inc(src_turned, R)
            pe.sem_inc(attr_turned, R)

            def front(i, r):
                n = R * i + r
                pe.wait_ge(loaded[r], 16 * (i + 1))
                pe.wait_ge(src_copied, n + 1)
                for q in range(4):
                    mm = pe.transpose(srow_ps[0:QUARTERS, q:W:4], rin[r][:, :, q * RW + EC], k.ident[:])
                mm.then_inc(src_turned, 1)
                pe.wait_ge(attr_copied, n + R + 1)
                pe.wait_ge(scanned, n + 1)
                for q in range(4):
                    mm = pe.transpose(attr_ps[r][:, q:W:4], attr[r][:, q, :], k.ident[:])
                mm.then_inc(attr_turned, 1)
                pe.wait_ge(src_copied, n + 2)
                pe.wait_ge(ids_ready, n + 1)
                pe.matmul(ids_ps[:], k.spread[:], srow[:], start=True, stop=True).then_inc(ids_spread, 1)

            pe.sem_inc(back_ready, R)

            def back(i, r):
                n = R * i + r
                pe.wait_ge(scanned, n + R + 1)
                pe.wait_ge(back_copied, n + 1)
                for q in range(4):
                    pe.transpose(mback[:, q * P:(q + 1) * P], mx[r][:, q:W:4], k.ident[:])
                for q in range(4):
                    mm = pe.transpose(sback[:, q * P:(q + 1) * P], sm[r][:, q:W:4], k.ident[:])
                mm.then_inc(back_ready, 1)

            front(0, 0)
            with pe.Fori(0, STEPS // R - 1) as i:
                for r in range(R):
                    front(i + (r + 1) // R, (r + 1) % R)
                    back(i, r)
            last = STEPS // R - 1
            for r in range(R):
                if r + 1 < R:
                    front(last, r + 1)
                back(last, r)

        @block.scalar
        def _(act):
            act.sem_inc(src_copied, 1)
            act.sem_inc(ids_ready, 1)
            act.sem_inc(back_copied, 1)
            act.wait_ge(init, 1)

            def front(i, r):
                n = R * i + r
                act.wait_ge(src_turned, n + R + 1)
                act.activation(srow[:], srow_ps[0:QUARTERS, :], ACT.Copy).then_inc(src_copied, 1)
                act.wait_ge(scanned, n + 1)
                act.wait_ge(ids_ready, n + 1)
                act.activation(ids[r][:, 0:1], ids[(r - 1) % R][:, W:W + 1], ACT.Copy)
                act.wait_ge(ids_spread, n + 1)
                act.activation(ids[r][:, 1:W + 1], ids_ps[:], ACT.Copy).then_inc(ids_ready, 1)

            def back(i, r, first=False):
                n = R * i + r
                act.wait_ge(back_ready, n + R + 1)
                if not first:
                    act.wait_ge(stored[r], 16 * i)
                act.activation(rout[r][:, :, :, 0:EC].rearrange("p g k c -> p k g c"),
                               mback[:].rearrange("p (k g c) -> p k g c", k=4, c=EC), ACT.Copy)
                act.activation(rout[r][:, :, :, EC:2 * EC].rearrange("p g k c -> p k g c"),
                               sback[:].rearrange("p (k g c) -> p k g c", k=4, c=EC), ACT.Copy).then_inc(back_copied, 1)
                act.wait_ge(back_copied, n + 2)
                act.dma_start(out_v[:, bass.ds(n, 1)], rout[r][:].rearrange("p g k c -> p g (k c)")[:, None])\
                    .then_inc(stored[r], 16)

            front(0, 0)
            for r in range(R):
                front((r + 1) // R, (r + 1) % R)
                back(0, r, first=True)
            with act.Fori(1, STEPS // R - 1) as i:
                for r in range(R):
                    front(i + (r + 1) // R, (r + 1) % R)
                    back(i, r)
            last = STEPS // R - 1
            for r in range(R):
                if r + 1 < R:
                    front(last, r + 1)
                back(last, r)
            for r in range(R):
                act.wait_ge(stored[r], 16 * (last + 1))

        @block.vector
        def _(dve):
            dve.memset(ids[R - 1][:], -1.0)
            dve.memset(mx[R - 1][:], -BIG)
            dve.memset(sm[R - 1][:], 0.0).then_inc(init, 1)
            dve.wait_ge(init, 1)
            dve.sem_inc(scanned, R)
            with dve.Fori(0, STEPS // R) as i:
                for r in range(R):
                    n = R * i + r
                    dve.wait_ge(ids_ready, n + 2)
                    dve.tensor_tensor(same[:], ids[r][:, 1:W + 1], ids[r][:, 0:W], ALU.is_equal).then_inc(flags, 1)
                    dve.wait_ge(flags, 2 * n + 1)
                    dve.tensor_scalar(bar[:], same[:], -1.0, BIG, ALU.add, ALU.mult).then_inc(flags, 1)
                    dve.wait_ge(flags, 2 * n + 2)
                    dve.wait_ge(attr_turned, n + R + 1)
                    dve.wait_ge(back_ready, n + 1)
                    dve.tensor_tensor_scan(mx[r][:], bar[:], attr_ps[r][:], mx[(r - 1) % R][:, W - 1:W], ALU.add, ALU.max)
                    dve.tensor_tensor_scan(sm[r][:], same[:], attr_ps[r][:], sm[(r - 1) % R][:, W - 1:W],
                                           ALU.mult, ALU.add).then_inc(scanned, 1)
                    dve.wait_ge(scanned, n + R + 1)


def norm(dve, step, k, z, out, mean, var, var_ready, std_ready, at):
    sq = k.sq
    step(dve.tensor_reduce(mean[:], z[:], AX.X, ALU.add))
    step(dve.tensor_scalar(mean[:], mean[:], 1.0 / C, None, ALU.mult))
    step(dve.tensor_tensor(z[:], z[:], b3(mean[:], C), ALU.subtract))
    step(dve.tensor_tensor(sq[:], z[:], z[:], ALU.mult))
    step(dve.tensor_reduce(var[:], sq[:], AX.X, ALU.add))
    dve.tensor_scalar(var[:], var[:], 1.0 / C, EPS, ALU.mult, ALU.add).then_inc(var_ready, 1)
    dve.wait_ge(std_ready, at)
    step(dve.reciprocal(var[:], var[:]))
    return dve.tensor_tensor(out[:], z[:], b3(var[:], C), ALU.mult)


def nodes(nc, k, d):
    NF = 3 * EC + 2
    CH = [range(4 * c, min(4 * c + 4, NT)) for c in range((NT + 3) // 4)]
    with ExitStack() as c:
        def sb(name, shape, dt=F32):
            return c.enter_context(nc.sbuf_tensor(name, shape, dt))

        def ps(name):
            return c.enter_context(nc.psum_tensor(name, [P, 512], F32))

        def sem(name):
            return c.enter_context(nc.semaphore(name))
        at_f, at_i, end = sb("at_f", [P, NT]), sb("at_i", [P, NT], I32), sb("end_n", [P, NT])
        run = sb("run", [P, NT, 2 * EC])
        seam = sb("seam", [P, QUARTERS - 1, 2 * EC])
        cross, bar, some, per = sb("cross", [P, NT]), sb("bar_n", [P, NT]), sb("some", [P, NT]), sb("per", [P, NT])
        tmp, feat = sb("tmp_n", [P, NT, EC]), sb("feat", [P, NT, NF])
        ft = [sb(f"ft{b}", [NF, 512]) for b in range(2)]
        h1 = [sb(f"h1_{b}", [HID, 512]) for b in range(2)]
        z, mean, var = sb("z", [P, NT, C]), sb("mean", [P, NT]), sb("var", [P, NT])
        attr_mean = sb("attr_mean", [EC, 1])
        ft_ps, h1_ps, y_ps, t_ps = ps("ft_ps"), ps("h1_ps"), ps("y_ps"), ps("t_ps")
        mean_ps, loop_ps = ps("mean_ps"), ps("loop_ps")
        at_ready, gathered, seam_in = sem("at_ready"), sem("gathered_n"), sem("seam_in")
        feat_ready, ft_turned, ft_ready, h1_done, h1_ready = sem("feat_ready"), sem("ft_turned"), sem("ft_ready"), sem("h1_done"), sem("h1_ready")
        y_done, y_used, dve_step, var_ready, std_ready = sem("y_done"), sem("y_used"), sem("nodes_dve"), sem("var_ready"), sem("std_ready")
        x_ready, x_turned, x_copied = sem("x_ready"), sem("x_turned"), sem("x_copied")
        sums_ready, mean_ready, attr_mean_ready, loop_ready = sem("sums_ready"), sem("mean_ready"), sem("attr_mean_ready"), sem("loop_ready")
        block = c.enter_context(nc.Block())

        @block.sync
        def _(sp):
            for g in range(QUARTERS - 1):
                row = (g + 1) * QROWS - 1
                sp.dma_start(seam[:, g, :], d.runs[row, :].partition_broadcast(P)).then_inc(seam_in, 16)

        @block.gpsimd
        def _(pool):
            pool.wait_ge(at_ready, 1)
            for i in range(NT):
                pool.indirect_dma_start(run[:, i, :], None, d.runs,
                                        bass.IndirectOffsetOnAxis(at_i[:, i:i + 1].bitcast(U32), 0)).then_inc(gathered, 16)

        @block.vector
        def _(dve):
            step = chain(dve, dve_step)
            step(dve.tensor_tensor(end[:], k.start_n[:], k.count_n[:], ALU.add))
            step(dve.tensor_scalar(at_f[:], end[:], -1.0, 0.0, ALU.add, ALU.max))
            dve.tensor_copy(at_i[:], at_f[:]).then_inc(at_ready, 1)
            dve.wait_ge(seam_in, 16 * (QUARTERS - 1))
            dve.wait_ge(gathered, 16 * NT)
            for g in range(QUARTERS - 1):
                row = float((g + 1) * QROWS)
                step(dve.tensor_scalar(cross[:], k.start_n[:], row, None, ALU.is_lt))
                step(dve.scalar_tensor_tensor(cross[:], end[:], row, cross[:], ALU.is_gt, ALU.mult))
                step(dve.tensor_scalar(bar[:], cross[:], -1.0, BIG, ALU.add, ALU.mult))
                step(dve.tensor_tensor(tmp[:], rep(seam[:, g, 0:EC], NT), b3(bar[:], EC), ALU.add))
                step(dve.tensor_tensor(run[:, :, 0:EC], run[:, :, 0:EC], tmp[:], ALU.max))
                step(dve.tensor_tensor(tmp[:], rep(seam[:, g, EC:2 * EC], NT), b3(cross[:], EC), ALU.mult))
                step(dve.tensor_tensor(run[:, :, EC:2 * EC], run[:, :, EC:2 * EC], tmp[:], ALU.add))
            dve.tensor_scalar(some[:], k.count_n[:], 0.0, None, ALU.is_gt)
            step(dve.tensor_scalar(per[:], k.count_n[:], 1.0, None, ALU.max))
            dve.tensor_tensor(feat[:, :, 0:EC], run[:, :, EC:2 * EC], b3(some[:], EC), ALU.mult)
            dve.tensor_tensor(feat[:, :, EC:2 * EC], run[:, :, 0:EC], b3(some[:], EC), ALU.mult)
            step(dve.reciprocal(per[:], per[:]))
            dve.tensor_copy(feat[:, :, 3 * EC:3 * EC + 1], k.u[:, 0:1].to_broadcast([P, NT])[:, :, None])
            dve.memset(feat[:, :, 3 * EC + 1:NF], 1.0)
            dve.tensor_tensor(feat[:, :, 2 * EC:3 * EC], feat[:, :, 0:EC], b3(per[:], EC), ALU.mult).then_inc(feat_ready, 1)
            dve.wait_ge(sums_ready, 1)
            dve.tensor_scalar(attr_mean[:], mean_ps[0:EC, 0:1], 1.0 / EDGES, None, ALU.mult).then_inc(attr_mean_ready, 1)
            dve.wait_ge(loop_ready, 1)
            dve.tensor_copy(k.loop_all[:], loop_ps[:, 0:LAYERS * C].rearrange("p (l n) -> p l n", l=LAYERS))
            dve.tensor_tensor(k.x[:], k.x[:], rep(k.b2[:], NT), ALU.add).then_inc(x_ready, 1)
            dve.wait_ge(x_ready, 1)
            for n, tiles in enumerate(CH):
                w = len(tiles)
                dve.wait_ge(y_done, n + 1)
                dve.tensor_tensor(z[:, tiles[0]:tiles[0] + w, :], k.x[:, tiles[0]:tiles[0] + w, :],
                                  y_ps[:, 0:w * C].rearrange("p (i n) -> p i n", n=C), ALU.add).then_inc(y_used, 1)
            dve.wait_ge(y_used, len(CH))
            norm(dve, step, k, z, k.x, mean, var, var_ready, std_ready, 1).then_inc(x_ready, 1)

        @block.scalar
        def _(act):
            for n, tiles in enumerate(CH):
                w = len(tiles) * P
                act.wait_ge(ft_turned, n + 1)
                act.activation(ft[n % 2][:, 0:w], ft_ps[0:NF, 0:w], ACT.Copy).then_inc(ft_ready, 1)
                act.wait_ge(h1_done, n + 1)
                act.activation(h1[n % 2][:, 0:w], h1_ps[:, 0:w], ACT.Relu).then_inc(h1_ready, 1)
            act.wait_ge(var_ready, 1)
            act.activation(var[:], var[:], ACT.Sqrt).then_inc(std_ready, 1)
            for n, tiles in enumerate(CH):
                w = len(tiles) * P
                act.wait_ge(x_turned, n + 1)
                act.activation(k.hT[0:C, tiles[0] * P:tiles[0] * P + w], t_ps[0:C, 0:w], ACT.Copy).then_inc(x_copied, 1)

        @block.tensor
        def _(pe):
            pe.wait_ge(feat_ready, 1)
            for i in range(NT):
                mm = pe.matmul(mean_ps[0:EC, 0:1], feat[:, i, 0:EC], k.ones[:, 0:1], start=(i == 0), stop=(i == NT - 1))
            mm.then_inc(sums_ready, 1)
            for n, tiles in enumerate(CH):
                w = len(tiles)
                if n:
                    pe.wait_ge(ft_ready, n)
                for j, i in enumerate(tiles):
                    mm = pe.transpose(ft_ps[0:NF, j * P:(j + 1) * P], feat[:, i, :], k.ident[:])
                mm.then_inc(ft_turned, 1)
                if n:
                    pe.wait_ge(h1_ready, n)
                pe.wait_ge(ft_ready, n + 1)
                pe.matmul(h1_ps[:, 0:w * P], k.w1[:], ft[n % 2][:, 0:w * P], start=True, stop=True).then_inc(h1_done, 1)
                if n:
                    pe.wait_ge(y_used, n)
                pe.wait_ge(h1_ready, n + 1)
                for j in range(w):
                    mm = pe.matmul(y_ps[:, j * C:(j + 1) * C], h1[n % 2][:, j * P:(j + 1) * P], k.w2[:],
                                   start=True, stop=True, skip_group_check=True)
                mm.then_inc(y_done, 1)
                if n == 0:
                    pe.wait_ge(attr_mean_ready, 1)
                    pe.matmul(loop_ps[:, 0:LAYERS * C], attr_mean[:].to_broadcast([EC, P]), k.wc[:],
                              start=True, stop=True).then_inc(loop_ready, 1)
            pe.wait_ge(x_ready, 2)
            for n, tiles in enumerate(CH):
                if n:
                    pe.wait_ge(x_copied, n)
                for j, i in enumerate(tiles):
                    mm = pe.transpose(t_ps[0:C, j * P:(j + 1) * P], k.x[:, i, :], k.ident[:])
                mm.then_inc(x_turned, 1)


def project(nc, k, d, s, l):
    with ExitStack() as c:
        pp = [c.enter_context(nc.psum_tensor(f"proj_ps{b}", [P, 512], F32)) for b in range(2)]
        CH = [range(4 * n, min(4 * n + 4, NT)) for n in range((NT + 3) // 4)]
        N = len(CH)
        block = c.enter_context(nc.Block())

        @block.scalar
        def _(act):
            act.activation(k.wlr[:], k.wlr_all[:, bass.ds(l, 1), :].rearrange("p a n -> p (a n)"), ACT.Copy).then_inc(s.weights_ready, 1)
            act.activation(k.bd[:], k.bd_all[:, bass.ds(l, 1), :].rearrange("p a n -> p (a n)"), ACT.Copy)
            for n, tiles in enumerate(CH):
                if n % 2:
                    w = len(tiles)
                    act.wait_ge(s.projected, N * l + n + 1)
                    act.activation(k.xlr[:, tiles[0]:tiles[0] + w, :],
                                   pp[1][:, 0:w * P].rearrange("p (i n) -> p i n", n=2 * C), ACT.Copy).then_inc(s.rows_ready_a, 1)

        @block.vector
        def _(dve):
            for to, of in ((k.att, k.att_all), (k.bias, k.bias_all), (k.loop, k.loop_all)):
                dve.tensor_copy(to[:], of[:, bass.ds(l, 1), :].rearrange("p a n -> p (a n)"))
            dve.tensor_copy(k.low[:], k.floor[:, bass.ds(l, 1)])
            for n, tiles in enumerate(CH):
                if n % 2 == 0:
                    w = len(tiles)
                    dve.wait_ge(s.projected, N * l + n + 1)
                    dve.tensor_copy(k.xlr[:, tiles[0]:tiles[0] + w, :],
                                    pp[0][:, 0:w * P].rearrange("p (i n) -> p i n", n=2 * C)).then_inc(s.rows_ready_v, 1)

        @block.tensor
        def _(pe):
            pe.wait_ge(s.weights_ready, l + 1)
            for n, tiles in enumerate(CH):
                if n >= 2:
                    if n % 2:
                        pe.wait_ge(s.rows_ready_a, (N // 2) * l + n // 2)
                    else:
                        pe.wait_ge(s.rows_ready_v, (N - N // 2) * l + n // 2)
                for j, i in enumerate(tiles):
                    mm = pe.matmul(pp[n % 2][:, j * P:(j + 1) * P], k.hT[0:C + 1, i * P:(i + 1) * P], k.wlr[:],
                                   start=True, stop=True, skip_group_check=True)
                mm.then_inc(s.projected, 1)

        @block.sync
        def _(sp):
            for n, tiles in enumerate(CH):
                if n % 2:
                    sp.wait_ge(s.rows_ready_a, (N // 2) * l + n // 2 + 1)
                else:
                    sp.wait_ge(s.rows_ready_v, (N - N // 2) * l + n // 2 + 1)
                t = slice(tiles[0], tiles[-1] + 1)
                for part, to in ((slice(0, C), d.xl_d), (slice(C, 2 * C), d.xr_d[0:NPAD, :])):
                    sp.dma_start(to.rearrange("(i p) n -> p i n", p=P)[:, t, :], k.xlr[:, t, part]).then_inc(s.rows_out, 16)
            sp.wait_ge(s.rows_out, 32 * N * (l + 1))
            alone(sp, k)


def finish(nc, k, d, s, l):
    CH = [range(4 * n, min(4 * n + 4, NT)) for n in range((NT + 3) // 4)]
    N = len(CH)
    with ExitStack() as c:
        def sb(name, shape, dt=F32):
            return c.enter_context(nc.sbuf_tensor(name, shape, dt))
        fp = [c.enter_context(nc.psum_tensor(f"fin_ps{b}", [P, 512], F32)) for b in range(2)]
        tp = [c.enter_context(nc.psum_tensor(f"hT_ps{b}", [P, 512], F32)) for b in range(2)]
        sums, el = sb("sums", [P, NT, SC]), sb("el", [P, NT, C])
        loop_s, top = sb("loop_s", [P, NT]), sb("top", [P, NT])
        w2, den = sb("w_pair", [P, 2, NT]), sb("den", [P, NT])
        block = c.enter_context(nc.Block())
        STEPS_F = 15

        @block.tensor
        def _(pe):
            for n, tiles in enumerate(CH):
                if n >= 2:
                    pe.wait_ge(s.sums_copied, N * l + n - 1)
                for j, i in enumerate(tiles):
                    mm = pe.transpose(fp[n % 2][:, j * SC:(j + 1) * SC], k.acc[0:SC, i * P:(i + 1) * P], k.ident[0:SC, 0:SC])
                mm.then_inc(s.sums_turned, 1)
            pe.wait_ge(s.h_ready, l + 1)
            alone(pe, k)
            for n, tiles in enumerate(CH):
                if n >= 2:
                    pe.wait_ge(s.h_copied, N * l + n - 1)
                    alone(pe, k)
                for j, i in enumerate(tiles):
                    mm = pe.transpose(tp[n % 2][0:C, j * P:(j + 1) * P], k.h[:, i, :], k.ident[:])
                mm.then_inc(s.h_turned, 1)

        @block.scalar
        def _(act):
            act.wait_ge(s.pair_ready, l + 1)
            act.activation(w2[:], w2[:], ACT.Exp).then_inc(s.pair_exp, 1)
            for n, tiles in enumerate(CH):
                w = len(tiles) * P
                act.wait_ge(s.h_turned, N * l + n + 1)
                act.activation(k.hT[0:C, tiles[0] * P:tiles[0] * P + w], tp[n % 2][0:C, 0:w], ACT.Copy).then_inc(s.h_copied, 1)

        @block.vector
        def _(dve):
            done = [0]

            def step(ins):
                done[0] += 1
                ins.then_inc(s.finish_step, 1)
                dve.wait_ge(s.finish_step, STEPS_F * l + done[0])
            xl, xr = k.xlr[:, :, 0:C], k.xlr[:, :, C:2 * C]
            step(dve.tensor_tensor(el[:], xl, xr, ALU.add))
            step(dve.tensor_tensor(el[:], el[:], rep(k.loop[:], NT), ALU.add))
            step(dve.scalar_tensor_tensor(el[:], el[:], NEG_SLOPE, el[:], ALU.mult, ALU.max))
            step(dve.tensor_tensor(el[:], el[:], rep(k.att[:], NT), ALU.mult))
            step(dve.tensor_reduce(loop_s[:], el[:], AX.X, ALU.add))
            for n, tiles in enumerate(CH):
                w = len(tiles)
                dve.wait_ge(s.sums_turned, N * l + n + 1)
                dve.tensor_copy(sums[:, tiles[0]:tiles[0] + w, :],
                                fp[n % 2][:, 0:w * SC].rearrange("p (i n) -> p i n", n=SC)).then_inc(s.sums_copied, 1)
            dve.wait_ge(s.sums_copied, N * (l + 1))
            shift = sums[:, :, SC - 1]
            step(dve.tensor_tensor(top[:], shift, loop_s[:], ALU.max))
            dve.tensor_tensor(w2[:, 0, :], shift, top[:], ALU.subtract)
            dve.tensor_tensor(w2[:, 1, :], loop_s[:], top[:], ALU.subtract).then_inc(s.pair_ready, 1)
            dve.wait_ge(s.pair_exp, l + 1)
            step(dve.tensor_tensor(den[:], sums[:, :, C], w2[:, 0, :], ALU.mult))
            step(dve.scalar_tensor_tensor(den[:], den[:], DEN_EPS, w2[:, 1, :], ALU.add, ALU.add))
            step(dve.reciprocal(den[:], den[:]))
            step(dve.tensor_tensor(w2[:], w2[:], den[:, None, :].to_broadcast([P, 2, NT]), ALU.mult))
            step(dve.tensor_tensor(k.h[:], sums[:, :, 0:C], b3(w2[:, 0, :], C), ALU.mult))
            step(dve.tensor_tensor(el[:], xl, b3(w2[:, 1, :], C), ALU.mult))
            step(dve.tensor_tensor(k.h[:], k.h[:], el[:], ALU.add))
            step(dve.tensor_tensor(k.h[:], k.h[:], rep(k.bias[:], NT), ALU.add))
            step(dve.tensor_scalar(k.h[:], k.h[:], k.low[:, 0:1], None, ALU.max))
            assert done[0] == STEPS_F
            dve.sem_inc(s.h_ready, 1)


def output(nc, k, d):
    with ExitStack() as c:
        mean, var = (c.enter_context(nc.sbuf_tensor(n, [P, NT], F32)) for n in ("mean_o", "var_o"))
        dve_step, var_ready, std_ready, z_ready, out_done = (
            c.enter_context(nc.semaphore(n)) for n in ("out_dve", "var_o_ready", "std_o_ready", "z_ready", "out_done"))
        block = c.enter_context(nc.Block())
        full = NODES // P

        @block.vector
        def _(dve):
            step = chain(dve, dve_step)
            step(dve.tensor_tensor(k.x[:], k.x[:], k.h[:], ALU.add))
            norm(dve, step, k, k.x, k.h, mean, var, var_ready, std_ready, 1).then_inc(z_ready, 1)

        @block.scalar
        def _(act):
            act.wait_ge(var_ready, 1)
            act.activation(var[:], var[:], ACT.Sqrt).then_inc(std_ready, 1)

        @block.sync
        def _(sp):
            sp.wait_ge(z_ready, 1)
            sp.dma_start(d.out[0:full * P, :].rearrange("(i p) n -> p i n", p=P), k.h[:, 0:full, :]).then_inc(out_done, 16)
            sp.dma_start(d.out[full * P:NODES, :], k.h[0:NODES - full * P, full, :]).then_inc(out_done, 16)
            sp.wait_ge(out_done, 32)


def edges(nc, k, d, s, l):
    R = 3
    SLOT = [(NG - r + R - 1) // R for r in range(R)]
    HALF = G // 2
    with ExitStack() as c:
        def sb(name, shape, dt=F32):
            return c.enter_context(nc.sbuf_tensor(name, shape, dt))

        def ps(name):
            return c.enter_context(nc.psum_tensor(name, [P, 512], F32))
        m = [sb(f"m{r}", [P, G, P]) for r in range(R)]
        mt = sb("mt", [P, G, P])
        xg = [sb(f"xg{r}", [P, G, C]) for r in range(R)]
        idx = [sb(f"idx{r}", [P, G], I32) for r in range(R)]
        xw = [sb(f"xw{r}", [P, G, C]) for r in range(R)]
        at = [sb(f"at{r}", [P, G // 4 * P]) for r in range(R)]
        e = sb("e", [P, G, C])
        score = [sb(f"score{r}", [P, G]) for r in range(R)]
        bar, last, first, run = sb("bar_e", [G, P]), sb("last", [G, P]), sb("first", [G, P]), sb("run_e", [G, P])
        ends, shift = sb("ends", [G, P]), sb("shift", [G, P])
        dif, wt, shift_out = sb("dif", [G, P + 1]), sb("wt", [G, P + 1]), sb("shift_out", [G, P])
        crow, cin_row, cin = sb("crow", [1, G + 1]), sb("cin_row", [1, G]), sb("cin", [G, 1])
        scale_d = sb("scale_d", [G, G])
        sw = sb("sw", [P, G, SC])
        rescale = sb("rescale", [SC, G])
        head = sb("head", [SC, G])
        m_ps = [ps(f"m_ps{b}") for b in range(2)]
        e_ps = [ps(f"e_ps{b}") for b in range(2)]
        agg_ps = [ps(f"agg_ps{b}") for b in range(2)]
        s_ps, w_ps = ps("s_ps"), ps("w_ps")
        st = s_ps[0:G, 0:P]
        cin_ps = s_ps[0:G, P:P + 1]
        top_row = w_ps[0:1, 0:G]
        wt_ps, sh_ps, res_ps = w_ps[:, 32:32 + G], w_ps[:, 64:64 + G], s_ps[0:SC, 256:256 + G]
        xr_windows = d.xr_d
        block = c.enter_context(nc.Block())

        def skewed(eng, a, b):
            if a:
                a(0, 0)
            with eng.Fori(0, (NG - 1) // R) as i:
                for r in range(R):
                    if a:
                        a(i + (r + 1) // R, (r + 1) % R)
                    if b:
                        b(i, r)
            if b:
                b((NG - 1) // R, 0)

        def N(i, r):
            return l * NG + i * R + r

        def nth(i, r):
            return l * SLOT[r] + i

        @block.sync
        def _(sp):
            def a(i, r):
                g = i * R + r
                for h in range(2):
                    _, base = nc.values_load_multi_w_load_instructions(
                        k.base_i[0:1, bass.ds(g * G + h * HALF, HALF)], engines=[ENG.SP], min_val=0, max_val=NODES,
                        skip_runtime_bounds_check_because=WIN)
                    if h == 0:
                        sp.wait_ge(s.e_ready, N(i, r) * 3 + 3)
                        sp.dma_start(at[r][:], d.attrt[:, bass.ds(g * (G // 4 * P), G // 4 * P)]).then_inc(s.at_in[r], 16)
                    for j in range(HALF):
                        sp.dma_start(xw[r][:, h * HALF + j, :], xr_windows[bass.ds(base[j], P), :]).then_inc(s.xw_in[r], 16)
            skewed(sp, a, None)

        @block.gpsimd
        def _(pool):
            def a(i, r):
                g = i * R + r
                pool.wait_ge(s.weighted, N(i, r) + 1)
                alone(pool, k)
                pool.tensor_copy(idx[r][:], k.src_i[:, bass.ds(g * G, G)]).then_inc(s.idx_ready, 1)
                pool.wait_ge(s.idx_ready, N(i, r) + 1)
                alone(pool, k)
                for j in range(G):
                    pool.indirect_dma_start(xg[r][:, j, :], None, d.xl_d,
                                            bass.IndirectOffsetOnAxis(idx[r][:, j:j + 1].bitcast(U32), 0))\
                        .then_inc(s.gathered[r], 16)
            skewed(pool, a, None)

        @block.vector
        def _(dve):
            def a(i, r):
                g, n = i * R + r, N(i, r)
                dve.wait_ge(s.agg_evacuated, n * 6 + 2)
                dve.tensor_tensor(m[r][:], rep(k.iota[:], G), b3(k.loc[:, bass.ds(g * G, G)], P), ALU.is_equal)\
                    .then_inc(s.m_ready, 1)
                dve.wait_ge(s.gathered[r], (nth(i, r) + 1) * (16 * G))
                for q in range(3):
                    dve.wait_ge(s.e_ready, n * 3 + q + 1 + 9)
                    dve.tensor_tensor(e[:, q * BAT:(q + 1) * BAT, :], e_ps[q % 2][:].rearrange("p (j n) -> p j n", n=C),
                                      xg[r][:, q * BAT:(q + 1) * BAT, :], ALU.add).then_inc(s.e_used, 1)
                dve.wait_ge(s.e_used, n * 3 + 3 + 2)
                dve.scalar_tensor_tensor(e[:], e[:], NEG_SLOPE, e[:], ALU.mult, ALU.max).then_inc(s.e_step, 1)
                dve.wait_ge(s.e_step, n * 2 + 1)
                dve.tensor_tensor(e[:], e[:], rep(k.att[:], G), ALU.mult).then_inc(s.e_step, 1)
                dve.wait_ge(s.e_step, n * 2 + 2)
                dve.tensor_reduce(score[r][:], e[:], AX.X, ALU.add).then_inc(s.score_ready, 1)

            def b(i, r):
                g, n = i * R + r, N(i, r)
                done = [0]
                ids = k.dstg[:, bass.ds(g * P, P)]

                def step(ins):
                    done[0] += 1
                    ins.then_inc(s.b_step, 1)
                    dve.wait_ge(s.b_step, n * 12 + done[0])
                step(dve.tensor_tensor(k.eq[:, 1:P], k.dstg[:, bass.ds(g * P + 1, P - 1)], k.dstg[:, bass.ds(g * P, P - 1)], ALU.is_equal))
                dve.tensor_scalar(bar[:], k.eq[:, 0:P], -1.0, BIG, ALU.add, ALU.mult)
                dve.tensor_scalar(last[:], k.eq[:, 1:P + 1], -1.0, 1.0, ALU.mult, ALU.add)
                step(dve.tensor_scalar(first[:], ids, k.dstg[:, bass.ds(g * P, 1)], -1.0, ALU.is_equal, ALU.add))
                dve.wait_ge(s.scores_turned, n + 1)
                dve.tensor_tensor_scan(run[:], bar[:], st, -BIG, ALU.add, ALU.max).then_inc(s.run_ready, 1)
                step(dve.tensor_copy(crow[:, 0:1], k.carry[:]))
                dve.wait_ge(s.top_turned, n + 1)
                step(dve.tensor_tensor_scan(crow[:, 1:G + 1], k.carry_b[:, bass.ds(g * G, G)], top_row, k.carry[:, 0:1],
                                            ALU.add, ALU.max))
                dve.tensor_tensor(cin_row[:], crow[:, 0:G], k.cont_b[:, bass.ds(g * G, G)], ALU.add).then_inc(s.cin_row_ready, 1)
                dve.tensor_copy(k.carry[:], crow[:, G:G + 1])
                step(dve.tensor_tensor(ends[:], run[:], last[:], ALU.mult))
                step(dve.tensor_tensor_scan(shift[:, ::-1], k.eq[:, 1:P + 1][:, ::-1], ends[:, ::-1], 0.0, ALU.mult, ALU.add))
                dve.wait_ge(s.cin_turned, n + 1)
                step(dve.tensor_copy(cin[:], cin_ps))
                step(dve.tensor_scalar(first[:], first[:], BIG, cin[:, 0:1], ALU.mult, ALU.add))
                step(dve.tensor_tensor(shift[:], shift[:], first[:], ALU.max))
                dve.tensor_tensor(shift_out[:], shift[:], last[:], ALU.mult)
                dve.tensor_tensor(dif[:, P:P + 1], cin[:], shift[:, 0:1], ALU.subtract)
                step(dve.tensor_tensor(dif[:, 0:P], st, shift[:], ALU.subtract))
                dve.sem_inc(s.dif_ready, 1)
                dve.wait_ge(s.weights_done, n + 1)
                step(dve.tensor_scalar(scale_d[:], k.ident[0:G, 0:G], wt[:, P:P + 1], None, ALU.mult))
                dve.sem_inc(s.scale_ready, 1)
                dve.wait_ge(s.weights_turned, n + 1)
                dve.wait_ge(s.agg_evacuated, n * 6 + 8)
                step(dve.tensor_copy(sw[:, :, C:SC], w_ps[:, 32:96].rearrange("p (a j) -> p j a", a=2)[:, 0:G, :]))
                assert done[0] == 12
                dve.tensor_tensor(sw[:, :, 0:C], xg[r][:], b3(sw[:, :, C], C), ALU.mult).then_inc(s.weighted, 1)
                base = []
                for h in range(2):
                    base += nc.values_load_multi_w_load_instructions(
                        k.base_i[0:1, bass.ds(g * G + h * HALF, HALF)], engines=[ENG.DVE], min_val=0, max_val=NODES,
                        skip_runtime_bounds_check_because=WIN)[1]
                for j in range(G):
                    if j % 4 == 0:
                        dve.wait_ge(s.agg_evacuated, n * 6 + j // 4 + 1 + 8)
                    col = k.acc[0:SC, bass.ds(base[j], 1)]
                    dve.scalar_tensor_tensor(col, col, rescale[:, j:j + 1], head[:, j:j + 1], ALU.mult, ALU.add)\
                        .then_inc(s.joined, 1)
                    dve.wait_ge(s.joined, n * G + j + 1)
                dve.sem_inc(s.joined_all, 1)
            skewed(dve, a, b)

        @block.scalar
        def _(act):
            def a(i, r):
                n = N(i, r)
                for b in range(G // 4):
                    if b % 2 == 0:
                        act.wait_ge(s.e_ready, n * 3 + b // 2 + 7)
                    act.wait_ge(s.m_turned, n * 6 + b + 1)
                    act.activation(mt[:, 4 * b:4 * b + 4, :], m_ps[b % 2][:].rearrange("p (j n) -> p j n", n=P), ACT.Copy)\
                        .then_inc(s.m_evacuated, 1)

            def b(i, r):
                g, n = i * R + r, N(i, r)
                act.wait_ge(s.dif_ready, n + 1)
                act.activation(wt[:], dif[:], ACT.Exp).then_inc(s.weights_done, 1)
                act.wait_ge(s.scale_turned, n + 1)
                act.wait_ge(s.joined_all, n + 1)
                act.activation(rescale[:], res_ps, ACT.Copy)
                for h in range(2):
                    _, base = nc.values_load_multi_w_load_instructions(
                        k.base_i[0:1, bass.ds(g * G + h * HALF, HALF)], engines=[ENG.Activation], min_val=0,
                        max_val=NODES, skip_runtime_bounds_check_because=WIN)
                    for q in range(3):
                        b4 = 3 * h + q
                        act.wait_ge(s.agg_ready, n * 6 + b4 + 1)
                        out = agg_ps[b4 % 2]
                        act.activation(head[:, 4 * b4:4 * b4 + 4], out[0:SC, 0:512:P], ACT.Copy)
                        for j in range(4):
                            act.wait_ge(s.window_done, n * G + 4 * b4 + j + 1)
                            alone(act, k)
                            act.activation(k.acc[0:SC, bass.ds(base[4 * q + j] + 1, P - 1)],
                                           out[0:SC, j * P + 1:(j + 1) * P], ACT.Copy).then_inc(s.window_done, 1)
                        act.wait_ge(s.window_done, n * G + 4 * b4 + 5)
                        act.sem_inc(s.agg_evacuated, 1)
            skewed(act, a, b)

        @block.tensor
        def _(pe):
            def turn(r, n, b):
                pe.wait_ge(s.m_evacuated, n * 6 + b + 1)
                for j in range(4):
                    mm = pe.transpose(m_ps[b % 2][:, j * P:(j + 1) * P], m[r][:, 4 * b + j, :], k.ident[:])
                mm.then_inc(s.m_turned, 1)

            def add_up(i, r, q):
                n = N(i, r)
                if q == 0:
                    pe.wait_ge(s.at_in[r], (nth(i, r) + 1) * 16)
                    pe.wait_ge(s.xw_in[r], (nth(i, r) + 1) * (16 * G))
                pe.wait_ge(s.e_used, n * 3 + (2, 1, 3)[q])
                pe.wait_ge(s.m_evacuated, n * 6 + 2 * q + 4)
                out = e_ps[q % 2]
                for h in range(2):
                    t = (2 * q + h) * P
                    pe.matmul(out[:, h * 256:(h + 1) * 256], at[r][:, t:t + P], k.bd[:], start=(h == 0), stop=False,
                              skip_group_check=True)
                for j in range(BAT):
                    mm = pe.matmul(out[:, j * C:(j + 1) * C], mt[:, q * BAT + j, :], xw[r][:, q * BAT + j, :],
                                   start=False, stop=(j == BAT - 1), skip_group_check=True)
                mm.then_inc(s.e_ready, 1)

            def a(i, r):
                n = N(i, r)
                pe.wait_ge(s.m_ready, n + 1)
                for b in range(4):
                    turn(r, n, b)
                add_up(i, r, 0)
                turn(r, n, 4)
                turn(r, n, 5)
                add_up(i, r, 1)
                add_up(i, r, 2)

            def b(i, r):
                n = N(i, r)
                pe.wait_ge(s.score_ready, n + 1)
                pe.transpose(st, score[r][:], k.ident[:]).then_inc(s.scores_turned, 1)
                pe.wait_ge(s.run_ready, n + 1)
                alone(pe, k)
                pe.transpose(top_row, run[:, P - 1:P], k.ident[0:G, 0:G]).then_inc(s.top_turned, 1)
                pe.wait_ge(s.cin_row_ready, n + 1)
                alone(pe, k)
                pe.matmul(cin_ps, cin_row[:], k.one[0:1, 0:1], start=True, stop=True, skip_group_check=True)\
                    .then_inc(s.cin_turned, 1)
                pe.wait_ge(s.weights_done, n + 1)
                alone(pe, k)
                pe.transpose(wt_ps, wt[:, 0:P], k.ident[0:G, 0:G])
                pe.transpose(sh_ps, shift_out[:], k.ident[0:G, 0:G]).then_inc(s.weights_turned, 1)
                pe.wait_ge(s.scale_ready, n + 1)
                pe.matmul(res_ps, k.sum_rows[:], scale_d[:], start=True, stop=True, skip_group_check=True)\
                    .then_inc(s.scale_turned, 1)
                pe.wait_ge(s.weighted, n + 1 + 3)
                for b4 in range(G // 4):
                    pe.wait_ge(s.agg_evacuated, n * 6 + b4 - 1 + 8)
                    for j in range(4):
                        t = 4 * b4 + j
                        mm = pe.matmul(agg_ps[b4 % 2][0:SC, j * P:(j + 1) * P], sw[:, t, :], m[r][:, t, :],
                                       start=True, stop=True, skip_group_check=True)
                    mm.then_inc(s.agg_ready, 1)
            skewed(pe, a, b)


def build(nc, d):
    with ExitStack() as c:
        k, s = Named(), Named()

        def sb(name, shape, dt=F32):
            return c.enter_context(nc.sbuf_tensor(name, shape, dt))

        def sem(name):
            return c.enter_context(nc.semaphore(name))
        k.src_i, k.base_i = sb("src_i", [P, T], I32), sb("base_i", [1, T], I32)
        k.x, k.h, k.xlr = sb("x", [P, NT, C]), sb("h", [P, NT, C]), sb("xlr", [P, NT, 2 * C])
        k.hT, k.acc = sb("hT", [C + 1, NPAD]), sb("acc", [P, ACCW])
        k.ident, k.iota, k.ones = sb("ident", [P, P]), sb("iota", [P, P]), sb("ones", [P, P])
        k.iota_b = sb("iota_b", [P, LO], BF16)
        k.loc, k.dstg = sb("loc", [P, T]), sb("dstg", [G, NG * P])
        k.cont_b, k.carry_b = sb("cont_b", [1, T]), sb("carry_b", [1, T])
        k.carry, k.one, k.eq = sb("carry", [1, 1]), sb("one", [1, 1]), sb("eq", [G, P + 1])
        k.sum_rows, k.floor = sb("sum_rows", [G, SC]), sb("floor", [P, LAYERS])
        k.wlr_all, k.bd_all = sb("wlr_all", [C + 1, LAYERS, 2 * C]), sb("bd_all", [P, LAYERS, QUARTERS * C])
        k.att_all, k.bias_all, k.loop_all = (sb(n, [P, LAYERS, C]) for n in ("att_all", "bias_all", "loop_all"))
        k.wlr, k.bd = sb("wlr", [C + 1, 2 * C]), sb("bd", [P, QUARTERS * C])
        k.att, k.bias, k.loop, k.low = sb("att", [P, C]), sb("bias", [P, C]), sb("loop", [P, C]), sb("low", [P, 1])
        k.start_n, k.count_n = sb("start_n", [P, NT]), sb("count_n", [P, NT])
        k.wc = sb("wc", [EC, LAYERS * C])
        k.passed = sem("passed")
        with ExitStack() as early:
            def sb1(name, shape, dt=F32):
                return early.enter_context(nc.sbuf_tensor(name, shape, dt))
            k.w1, k.w2, k.b2, k.u = sb1("w1", [3 * EC + 2, HID]), sb1("w2", [HID, C]), sb1("b2", [P, C]), sb1("u", [P, 1])
            k.sq, k.spread = sb1("sq", [P, NT, C]), sb1("spread", [QUARTERS, P])
            with ExitStack() as sorting:
                def sb2(name, shape, dt=F32):
                    return sorting.enter_context(nc.sbuf_tensor(name, shape, dt))
                k.hi, k.lo = sb2("hi", [P, T]), sb2("lo", [P, T])
                k.earlier, k.upper = sb2("earlier", [P, P]), sb2("upper", [HI, HI])
                k.count_ring = [sb2(f"count_ring{u}", [HI, G, LO]) for u in range(2)]
                setup(nc, k, d)
                histogram(nc, k, d)
                sort(nc, k, d)
            scan(nc, k, d)
            nodes(nc, k, d)
        s.weights_ready, s.projected, s.rows_ready_a, s.rows_ready_v = sem("weights_ready"), sem("projected"), sem("rows_ready_a"), sem("rows_ready_v")
        s.rows_out, s.sums_turned, s.sums_copied, s.h_ready = sem("rows_out"), sem("sums_turned"), sem("sums_copied"), sem("h_ready")
        s.h_turned, s.h_copied, s.pair_ready, s.pair_exp = sem("h_turned"), sem("h_copied"), sem("pair_ready"), sem("pair_exp")
        s.finish_step, s.m_ready, s.m_turned, s.m_evacuated = sem("finish_step"), sem("m_ready"), sem("m_turned"), sem("m_evacuated")
        s.e_ready, s.e_used, s.e_step, s.score_ready = sem("e_ready"), sem("e_used"), sem("e_step"), sem("score_ready")
        s.scores_turned, s.run_ready, s.top_turned, s.cin_row_ready = sem("scores_turned"), sem("run_ready"), sem("top_turned"), sem("cin_row_ready")
        s.cin_turned, s.dif_ready, s.weights_done, s.weights_turned = sem("cin_turned"), sem("dif_ready"), sem("weights_done"), sem("weights_turned")
        s.scale_ready, s.scale_turned, s.weighted, s.b_step = sem("scale_ready"), sem("scale_turned"), sem("weighted"), sem("b_step")
        s.agg_ready, s.agg_evacuated, s.window_done, s.joined = sem("agg_ready"), sem("agg_evacuated"), sem("window_done"), sem("joined")
        s.joined_all, s.idx_ready = sem("joined_all"), sem("idx_ready")
        s.at_in, s.xw_in, s.gathered = ([sem(f"{n}{r}") for r in range(3)] for n in ("at_in", "xw_in", "gathered"))
        with nc.Block() as block:
            @block.sync
            def _(sp):
                sp.sem_inc(s.m_evacuated, 2)
                sp.sem_inc(s.e_used, 2)
                sp.sem_inc(s.e_ready, 9)
                sp.sem_inc(s.weighted, 3)
                sp.sem_inc(s.agg_evacuated, 8)
                sp.sem_inc(s.joined_all, 1)
                sp.sem_inc(s.window_done, 1)
        with nc.Fori(0, LAYERS) as l:
            project(nc, k, d, s, l)
            edges(nc, k, d, s, l)
            finish(nc, k, d, s, l)
        k.sq = c.enter_context(nc.sbuf_tensor("sq_o", [P, NT, C], F32))
        output(nc, k, d)


def kernel(**inputs):
    import numpy as np
    import concourse.bacc as bacc
    from concourse.bass_utils import run_bass_kernel_spmd

    nc = bacc.Bacc("TRN2", target_bir_lowering=False, num_devices=1)
    a = {n: np.asarray(v) for n, v in inputs.items()}
    pad = ROWS - EDGES

    def tiles(v):
        return np.ascontiguousarray(np.pad(v, (0, pad), constant_values=NODES).reshape(T, P).T)
    attr = np.pad(a["edge_attr_32"], ((0, pad), (0, 0))).reshape(T, P, EC)
    dst = np.pad(a["dst"], (0, pad), constant_values=NODES)
    arrays = dict(
        src=tiles(a["src"]), dst=tiles(a["dst"]),
        dstg=dst.reshape(NG, G, P).transpose(1, 0, 2).reshape(G, NG * P),
        attr=attr.transpose(1, 0, 2),
        attrt=attr.reshape(T // 4, 4, P, EC).transpose(1, 3, 0, 2).reshape(P, T // 4 * P),
        x=np.pad(a["x"], ((0, NPAD - NODES), (0, 0))).reshape(NT, P, C).transpose(1, 0, 2),
        w1=a["L0_gnn_W1"], b1=a["L0_gnn_b1"], w2=a["L0_gnn_W2"], b2=a["L0_gnn_b2"], u=a["L0_gnn_u"],
        wembt=a["L1_gnn_W_emb"].T, bemb=a["L1_gnn_b_emb"].reshape(C, 1), wl=a["L1_gnn_Wl"], bl=a["L1_gnn_bl"],
        wr=a["L1_gnn_Wr"], br=a["L1_gnn_br"], we=a["L1_gnn_We"], att=a["L1_gnn_att"], bias=a["L1_gnn_bias"])
    arrays = {n: np.ascontiguousarray(v) for n, v in arrays.items()}
    def given(name):
        v = arrays[name]
        return nc.dram_tensor(f"in_{name}", v.shape, mybir.dt.from_np(v.dtype), kind="ExternalInput").ap()
    d = Named()
    d.src, d.dst, d.dstg, d.attr = given("src"), given("dst"), given("dstg"), given("attr")
    d.attrt, d.x, d.w1, d.b1 = given("attrt"), given("x"), given("w1"), given("b1")
    d.w2, d.b2, d.u, d.wembt = given("w2"), given("b2"), given("u"), given("wembt")
    d.bemb, d.wl, d.bl, d.wr = given("bemb"), given("wl"), given("bl"), given("wr")
    d.br, d.we, d.att, d.bias = given("br"), given("we"), given("att"), given("bias")
    d.out = nc.dram_tensor("out", (NODES, C), F32, kind="ExternalOutput").ap()
    d.tables = nc.dram_tensor("tables", (2, NPAD), F32).ap()
    d.sorted = nc.dram_tensor("sorted", (ROWS, RW), F32).ap()
    d.runs = nc.dram_tensor("runs", (ROWS, 2 * EC), F32).ap()
    d.xl_d, d.xr_d = nc.dram_tensor("xl_d", (NPAD, C), F32).ap(), nc.dram_tensor("xr_d", (NPAD + P, C), F32).ap()
    build(nc, d)
    r = run_bass_kernel_spmd(nc, [{f"in_{n}": v for n, v in arrays.items()}], core_ids=[0])
    return r.results[0]["out"]
```

```python
from contextlib import ExitStack

import concourse.bass as bass
import concourse.mybir as mybir

F32, BF16, I32, U32 = mybir.dt.float32, mybir.dt.bfloat16, mybir.dt.int32, mybir.dt.uint32
ALU, ACT, AX = mybir.AluOpType, mybir.ActivationFunctionType, mybir.AxisListType
ENG = mybir.EngineType

P = 128
NODES, EDGES = 3125, 103125
EC, C, HID, LAYERS = 32, 64, 128, 3
G = 24
NG = 34
T = G * NG
ROWS = T * P
NT = 25
NPAD = NT * P
ACCW = NPAD + P
LO = 64
HI = NPAD // LO
HL = HI + LO
RW = EC + 1
QUARTERS = 4
STEPS = T // QUARTERS // 4
QROWS = ROWS // QUARTERS
BAT = 8
SC = C + 2
BIG = 1e30
NEG_SLOPE, EPS, DEN_EPS = 0.2, 1e-5, 1e-16
WIN = "node ids lie in [0, 3125]"


class Named:
    pass


def b3(ap, n):
    return ap[:, :, None].to_broadcast([ap.shape[0], ap.shape[1], n])


def rep(ap, n):
    return ap[:, None, :].to_broadcast([ap.shape[0], n, ap.shape[1]])


def alone(eng, k):
    eng.sem_inc(k.passed, 1)


def chain(eng, sem):
    count = [0]

    def run(ins):
        count[0] += 1
        ins.then_inc(sem, 1)
        eng.wait_ge(sem, count[0])
    return run


def setup(nc, k, d):
    with ExitStack() as c:
        def sb(name, shape, dt=F32):
            return c.enter_context(nc.sbuf_tensor(name, shape, dt))

        def sem(name):
            return c.enter_context(nc.semaphore(name))
        iota_i = sb("iota_i", [P, P], I32)
        hi_i, lo_i = sb("hi_i", [P, T], I32), sb("lo_i", [P, T], I32)
        dst_i = sb("dst_i", [P, T], I32)
        last_i = sb("last_i", [1, T], I32)
        last_f, single = sb("last_f", [1, T]), sb("single_row", [1, T])
        dst_f = sb("dst_f", [P, T])
        emb4, embx = sb("emb4", [C, P]), sb("embx", [C, C + 1])
        we = sb("we", [C, LAYERS, C])
        ids_in, weights_in = sem("ids_in"), sem("weights_in")
        pool_step, dve_step, const_ready = sem("setup_pool"), sem("setup_dve"), sem("const_ready")
        dstf_ready, base_ready, wc_ready = sem("dstf_ready"), sem("base_ready"), sem("wc_ready")
        zero_ready, zero_out = sem("zero_ready"), sem("zero_out")
        base_ps = [c.enter_context(nc.psum_tensor(f"base_ps{h}", [P, 512], F32)) for h in range(2)]
        last_ps = [c.enter_context(nc.psum_tensor(f"last_ps{h}", [P, 512], F32)) for h in range(2)]
        wc_ps = c.enter_context(nc.psum_tensor("wc_ps", [P, 512], F32))
        wx_ps = c.enter_context(nc.psum_tensor("wx_ps", [P, 512], F32))
        block = c.enter_context(nc.Block())

        @block.sync
        def _(sp):
            sp.dma_start(k.src_i[:], d.src).then_inc(ids_in, 16)
            sp.dma_start(dst_i[:], d.dst).then_inc(ids_in, 16)
            sp.dma_start(last_i[:], d.dst[P - 1:P, :]).then_inc(ids_in, 16)
            sp.dma_start(k.base_i[:], d.dst[0:1, :]).then_inc(ids_in, 16)
            sp.dma_start(k.x[:], d.x).then_inc(weights_in, 16)
            sp.dma_start(k.w1[0:97, :], d.w1).then_inc(weights_in, 16)
            sp.dma_start(k.w1[97:98, :], d.b1[None, :]).then_inc(weights_in, 16)
            sp.dma_start(k.w2[:], d.w2).then_inc(weights_in, 16)
            sp.dma_start(k.b2[:], d.b2.partition_broadcast(P)).then_inc(weights_in, 16)
            sp.dma_start(k.u[:], d.u[0].partition_broadcast(P)).then_inc(weights_in, 16)
            sp.dma_start(k.att_all[:], d.att.partition_broadcast(P)).then_inc(weights_in, 16)
            sp.dma_start(k.bias_all[:], d.bias.partition_broadcast(P)).then_inc(weights_in, 16)
            sp.dma_start(k.biast[:], d.biast).then_inc(weights_in, 16)
            sp.dma_start(k.wlr_all[0:C, :, 0:C], d.wl.rearrange("l c n -> c l n")).then_inc(weights_in, 16)
            sp.dma_start(k.wlr_all[0:C, :, C:2 * C], d.wr.rearrange("l c n -> c l n")).then_inc(weights_in, 16)
            sp.dma_start(k.wlr_all[C:C + 1, :, 0:C], d.bl[None]).then_inc(weights_in, 16)
            sp.dma_start(k.wlr_all[C:C + 1, :, C:2 * C], d.br[None]).then_inc(weights_in, 16)
            sp.dma_start(we[:], d.we.rearrange("l c n -> c l n")).then_inc(weights_in, 16)
            sp.wait_ge(zero_ready, 1)
            for q in range(QUARTERS):
                sp.dma_start(emb4[:, EC * q:EC * (q + 1)], d.wembt).then_inc(weights_in, 16)
            sp.dma_start(embx[:, C:C + 1], d.bemb).then_inc(weights_in, 16)
            sp.wait_ge(zero_ready, 2)
            sp.dma_start(d.xr_d[NPAD:NPAD + P, :], k.acc[:, 0:C]).then_inc(zero_out, 16)
            sp.wait_ge(zero_out, 16)

        @block.gpsimd
        def _(pool):
            pool.iota(iota_i[:], [[1, P]], base=0, channel_multiplier=0).then_inc(const_ready, 1)
            pool.memset(embx[:], 0.0).then_inc(zero_ready, 1)
            pool.memset(k.acc[:], 0.0).then_inc(zero_ready, 1)
            pool.memset(k.ident[:], 0.0).then_inc(pool_step, 1)
            pool.memset(k.earlier[:], 1.0).then_inc(pool_step, 1)
            pool.memset(k.upper[:], 1.0).then_inc(pool_step, 1)
            pool.memset(k.spread[:], 1.0).then_inc(pool_step, 1)
            pool.memset(k.sum_rows[:], 0.0).then_inc(pool_step, 1)
            pool.wait_ge(pool_step, 5)
            pool.affine_select(out=k.ident[:], in_=k.ident[:], compare_op=ALU.not_equal, fill=1.0, base=0,
                               pattern=[[-1, P]], channel_multiplier=1).then_inc(const_ready, 1)
            pool.affine_select(out=k.earlier[:], in_=k.earlier[:], compare_op=ALU.is_gt, fill=0.0, base=0,
                               pattern=[[-1, P]], channel_multiplier=1).then_inc(const_ready, 1)
            pool.affine_select(out=k.upper[:], in_=k.upper[:], compare_op=ALU.is_gt, fill=0.0, base=0,
                               pattern=[[1, HI]], channel_multiplier=-1).then_inc(const_ready, 1)
            pool.affine_select(out=k.spread[:], in_=k.spread[:], compare_op=ALU.is_ge, fill=0.0, base=0,
                               pattern=[[1, P]], channel_multiplier=-EC).then_inc(pool_step, 1)
            pool.wait_ge(pool_step, 6)
            pool.affine_select(out=k.spread[:], in_=k.spread[:], compare_op=ALU.is_ge, fill=0.0, base=EC - 1,
                               pattern=[[-1, P]], channel_multiplier=EC).then_inc(const_ready, 1)
            pool.memset(k.ones[:], 1.0).then_inc(const_ready, 1)
            pool.memset(k.sum_rows[:, 0:SC - 1], 1.0).then_inc(const_ready, 1)
            pool.memset(k.hT[:], 1.0).then_inc(const_ready, 1)
            pool.memset(k.bd_all[:], 0.0).then_inc(const_ready, 1)

        @block.vector
        def _(dve):
            step = chain(dve, dve_step)
            dve.wait_ge(ids_in, 64)
            dve.tensor_copy(dst_f[:], dst_i[:])
            dve.tensor_copy(last_f[:], last_i[:]).then_inc(dstf_ready, 1)
            dve.tensor_scalar(hi_i[:], k.src_i[:], 6, None, ALU.logical_shift_right)
            step(dve.tensor_scalar(lo_i[:], k.src_i[:], LO - 1, None, ALU.bitwise_and))
            dve.tensor_copy(k.hi[:], hi_i[:])
            dve.tensor_copy(k.lo[:], lo_i[:])
            step(dve.memset(k.cont_b[:], 0.0))
            dve.tensor_tensor(k.cont_b[:, 1:T], dst_f[0:1, 1:T], last_f[:, 0:T - 1], ALU.is_equal)
            step(dve.tensor_tensor(single[:], dst_f[0:1, :], last_f[:], ALU.is_equal))
            step(dve.tensor_tensor(k.carry_b[:], k.cont_b[:], single[:], ALU.mult))
            dve.tensor_scalar(k.cont_b[:], k.cont_b[:], -1.0, BIG, ALU.add, ALU.mult)
            dve.tensor_scalar(k.carry_b[:], k.carry_b[:], -1.0, BIG, ALU.add, ALU.mult)
            dve.memset(k.carry[:], -BIG)
            dve.memset(k.partial[:], 0.0)
            dve.memset(k.eq[:], 0.0)
            dve.memset(k.one[:], 1.0)
            dve.wait_ge(const_ready, 9)
            step(dve.tensor_copy(k.iota[:], iota_i[:]))
            step(dve.tensor_copy(k.iota_b[:], k.iota[:, 0:LO]))
            dve.wait_ge(base_ready, 1)
            for h in range(2):
                dve.tensor_tensor(k.loc[:, h * T // 2:(h + 1) * T // 2], dst_f[:, h * T // 2:(h + 1) * T // 2],
                                  base_ps[h][:, 0:T // 2], ALU.subtract)
                half = slice(h * T // 2, (h + 1) * T // 2)
                dve.tensor_tensor(k.in_last[:, half], dst_f[:, half], last_ps[h][:, 0:T // 2], ALU.is_equal)
                step(dve.tensor_copy(k.single[:, half], base_ps[h][0:SC, 0:T // 2]))
                step(dve.tensor_tensor(k.single[:, half], k.single[:, half], last_ps[h][0:SC, 0:T // 2], ALU.is_equal))
            dve.wait_ge(wc_ready, 1)
            dve.tensor_copy(k.wc[:], wc_ps[0:EC, 0:LAYERS * C])
            for q in range(QUARTERS):
                s = slice(EC * q, EC * (q + 1))
                dve.tensor_copy(k.bd_all[s, :, q * C:(q + 1) * C],
                                wc_ps[s, 0:LAYERS * C].rearrange("p (l n) -> p l n", l=LAYERS))
            brow = k.wlr_all[C:C + 1, :, C:2 * C]
            step(dve.tensor_tensor(brow, brow, wx_ps[C:C + 1, 0:LAYERS * C].rearrange("p (l n) -> p l n", l=LAYERS),
                                   ALU.add))

        @block.tensor
        def _(pe):
            pe.wait_ge(dstf_ready, 1)
            pe.wait_ge(const_ready, 9)
            for h in range(2):
                half = slice(h * T // 2, (h + 1) * T // 2)
                pe.matmul(base_ps[h][:, 0:T // 2], k.ones[0:1, 0:P], dst_f[0:1, half], start=True, stop=True)
                mm = pe.matmul(last_ps[h][:, 0:T // 2], k.ones[0:1, 0:P], last_f[:, half], start=True, stop=True)
            mm.then_inc(base_ready, 1)
            pe.wait_ge(weights_in, 16 * 19)
            pe.matmul(wc_ps[:, 0:LAYERS * C], emb4[:], we[:].rearrange("p l n -> p (l n)"), start=True, stop=True)
            pe.matmul(wx_ps[0:C + 1, 0:LAYERS * C], embx[:], we[:].rearrange("p l n -> p (l n)"),
                      start=True, stop=True).then_inc(wc_ready, 1)


def one_hots(nc, dve, k, oh, t0):
    dve.tensor_tensor(oh[:, :, 0:HI], rep(k.iota_b[:, 0:HI], G), b3(k.hi[:, bass.ds(t0, G)], HI), ALU.is_equal)
    return dve.tensor_tensor(oh[:, :, HI:HL], rep(k.iota_b[:], G), b3(k.lo[:, bass.ds(t0, G)], LO), ALU.is_equal)


def histogram(nc, k, d):
    with ExitStack() as c:
        def sb(name, shape, dt=F32):
            return c.enter_context(nc.sbuf_tensor(name, shape, dt))

        def sem(name):
            return c.enter_context(nc.semaphore(name))
        oh = [sb(f"oh_h{u}", [P, HL, G], BF16) for u in range(2)]
        values = sb("values", [P, HL, G], BF16)
        counts, upto, rows_of = sb("counts", [HI, LO]), sb("upto", [HI, LO]), sb("node_rows", [NT, 2, P])
        oh_ready, oh_used, counted = sem("oh_ready"), sem("oh_used"), sem("counted")
        upto_ready, off_ready, dve_step, table_ready = sem("upto_ready"), sem("off_ready"), sem("hist_dve"), sem("table_ready")
        table_out, table_in, turned = sem("table_out"), sem("table_in"), sem("turned")
        cps = c.enter_context(nc.psum_tensor("counts_ps", [P, 512], F32))
        ops = c.enter_context(nc.psum_tensor("offset_ps", [P, 512], F32))
        block = c.enter_context(nc.Block())

        @block.vector
        def _(dve):
            step = chain(dve, dve_step)
            dve.tensor_copy(values[:, 0:HI, :], b3(k.iota_b[:, 0:HI], G))
            step(dve.tensor_copy(values[:, HI:HL, :], b3(k.iota_b[:], G)))
            with dve.Fori(0, NG // 2) as i:
                for u in range(2):
                    t = bass.ds((2 * i + u) * G, G)
                    dve.wait_ge(oh_used, 2 * i + u + 1)
                    dve.tensor_tensor(oh[u][:, 0:HI, :], values[:, 0:HI, :], rep(k.hi[:, t], HI), ALU.is_equal)
                    dve.tensor_tensor(oh[u][:, HI:HL, :], values[:, HI:HL, :], rep(k.lo[:, t], LO), ALU.is_equal)\
                        .then_inc(oh_ready, 1)
            dve.wait_ge(counted, 1)
            step(dve.tensor_copy(counts[:], cps[0:HI, 0:LO]))
            dve.tensor_tensor_scan(upto[:], k.ones[0:HI, 0:LO], counts[:], 0.0, ALU.mult, ALU.add).then_inc(upto_ready, 1)
            dve.wait_ge(upto_ready, 1)
            dve.wait_ge(off_ready, 1)
            step(dve.tensor_tensor(upto[:], upto[:], counts[:], ALU.subtract))
            dve.tensor_scalar(k.count_ring[0][:, 0, :], upto[:], ops[0:HI, 0:1], None, ALU.add).then_inc(table_ready, 1)
            dve.wait_ge(turned, 1)
            dve.tensor_copy(k.start_n[:], ops[:, 64:64 + NT])
            dve.tensor_copy(k.count_n[:], ops[:, 128:128 + NT])

        @block.tensor
        def _(pe):
            pe.matmul(cps[0:HI, 0:LO], k.sum_rows[0:1, SC - 1:SC].to_broadcast([1, HI]),
                      k.ones[0:1, 0:LO], start=True, stop=False, skip_group_check=True)
            pe.sem_inc(oh_used, 2)
            with pe.Fori(0, NG // 2) as i:
                for u in range(2):
                    pe.wait_ge(oh_ready, 2 * i + u + 1)
                    for j in range(G):
                        mm = pe.matmul(cps[0:HI, 0:LO], oh[u][:, 0:HI, j], oh[u][:, HI:HL, j],
                                       start=False, stop=False, skip_group_check=True)
                    mm.then_inc(oh_used, 1)
            pe.wait_ge(oh_used, NG + 2)
            pe.matmul(cps[0:HI, 0:LO], k.sum_rows[0:1, SC - 1:SC].to_broadcast([1, HI]),
                      k.ones[0:1, 0:LO], start=False, stop=True, skip_group_check=True).then_inc(counted, 1)
            pe.wait_ge(upto_ready, 1)
            pe.matmul(ops[0:HI, 0:1], k.upper[:], upto[:, LO - 1:LO], start=True, stop=True).then_inc(off_ready, 1)
            pe.wait_ge(table_in, 32)
            pe.wait_ge(table_ready, 1)
            pe.transpose(ops[:, 64:64 + NT], rows_of[:, 0, :], k.ident[0:NT, 0:NT])
            pe.transpose(ops[:, 128:128 + NT], rows_of[:, 1, :], k.ident[0:NT, 0:NT]).then_inc(turned, 1)

        @block.sync
        def _(sp):
            sp.wait_ge(table_ready, 1)
            sp.dma_start(d.tables[0].rearrange("(h l) -> h l", l=LO), k.count_ring[0][:, 0, :]).then_inc(table_out, 16)
            sp.dma_start(d.tables[1].rearrange("(h l) -> h l", l=LO), counts[:]).then_inc(table_out, 16)
            sp.wait_ge(table_out, 32)
            for m in range(2):
                sp.dma_start(rows_of[:, m, :], d.tables[m].rearrange("(i p) -> i p", p=P)).then_inc(table_in, 16)


def sort(nc, k, d):
    with ExitStack() as c:
        def sb(name, shape, dt=F32):
            return c.enter_context(nc.sbuf_tensor(name, shape, dt))

        def ps(name, dt=F32, n=512):
            return c.enter_context(nc.psum_tensor(name, [P, n], dt))

        def sem(name):
            return c.enter_context(nc.semaphore(name))
        oh = [sb(f"oh_s{u}", [P, G, HL], BF16) for u in range(2)]
        rows = [sb(f"rows{u}", [P, G, RW]) for u in range(2)]
        place = [sb(f"place{u}", [P, G], I32) for u in range(2)]
        hi_t = sb("hi_t", [HI, BAT, P])
        same, picked = sb("same", [P, BAT, P]), sb("picked", [P, BAT, LO])
        rank, before = sb("rank", [P, BAT]), sb("before", [P, BAT])
        ident_b = sb("ident_b", [P, P], BF16)
        hp = ps("hi_ps", BF16, BAT * P)
        dp, lp = ps("delta_ps"), ps("lookup_ps")
        bp = [ps(f"source_ps{n}") for n in range(2)]
        rows_in = [sem(f"rows_in{u}") for u in range(2)]
        scattered = [sem(f"scattered{u}") for u in range(2)]
        oh_ready, src_ready, place_ready, ident_ready = sem("s_oh_ready"), sem("src_ready"), sem("place_ready"), sem("ident_ready")
        hi_turned, hi_ready, delta_ready, ring_ready = sem("hi_turned"), sem("hi_ready"), sem("delta_ready"), sem("ring_ready")
        source_ready, source_used, found, found_used = sem("source_ready"), sem("source_used"), sem("found"), sem("found_used")
        picked_ready, before_ready, rows_free = sem("picked_ready"), sem("before_ready"), sem("rows_free")
        block = c.enter_context(nc.Block())
        B3 = G // BAT

        @block.sync
        def _(sp):
            with sp.Fori(0, NG // 2) as i:
                for u in range(2):
                    g = 2 * i + u
                    sp.wait_ge(rows_free, g + 1)
                    sp.dma_start(rows[u][:, :, 0:EC], d.attr[:, bass.ds(g * G, G), :]).then_inc(rows_in[u], 16)

        @block.gpsimd
        def _(pool):
            pool.sem_inc(rows_free, 2)

            def both(i, first):
                for u in range(2):
                    at_once = first and u == 0
                    if not at_once:
                        pool.wait_ge(place_ready, B3 * (2 * i + u + 1))
                    pool.wait_ge(rows_in[u], 16 * (i + 1))
                    alone(pool, k)
                    for j in range(G):
                        if at_once and j % BAT == 0:
                            pool.wait_ge(place_ready, j // BAT + 1)
                        if j == BAT and not (first and u == 0):
                            pool.wait_ge(scattered[1 - u], 16 * G * (i + u))
                            pool.sem_inc(rows_free, 1)
                        pool.indirect_dma_start(
                            d.sorted, bass.IndirectOffsetOnAxis(place[u][:, j:j + 1].bitcast(U32), 0),
                            rows[u][:, j, :], None).then_inc(scattered[u], 16)

            both(0, True)
            with pool.Fori(1, NG // 2) as i:
                both(i, False)
            pool.wait_ge(scattered[1], 16 * G * (NG // 2))

        @block.vector
        def _(dve):
            dve.tensor_copy(ident_b[:], k.ident[:]).then_inc(ident_ready, 1)
            with dve.Fori(0, NG // 2) as i:
                for u in range(2):
                    g = 2 * i + u
                    one_hots(nc, dve, k, oh[u], g * G).then_inc(oh_ready, 1)
                    dve.wait_ge(rows_free, g + 1)
                    dve.scalar_tensor_tensor(rows[u][:, :, EC], k.hi[:, bass.ds(g * G, G)], float(LO),
                                             k.lo[:, bass.ds(g * G, G)], ALU.mult, ALU.add).then_inc(src_ready, 1)
                    for q in range(B3):
                        b = B3 * g + q
                        dve.wait_ge(delta_ready, b + 1)
                        for j in range(BAT):
                            t = q * BAT + j
                            now = k.count_ring[u][:, t, :]
                            after = k.count_ring[u][:, t + 1, :] if t + 1 < G else k.count_ring[1 - u][:, 0, :]
                            if j:
                                dve.wait_ge(ring_ready, BAT * b + j)
                            dve.tensor_tensor(after, now, dp[0:HI, j * LO:(j + 1) * LO], ALU.add).then_inc(ring_ready, 1)
                        for j in range(BAT):
                            if j % 4 == 0:
                                dve.wait_ge(source_ready, 2 * b + j // 4 + 1)
                            ins = dve.scalar_tensor_tensor(
                                same[:, j, :], bp[j // 4][:, (j % 4) * P:(j % 4 + 1) * P],
                                rows[u][:, q * BAT + j, EC:EC + 1], k.earlier[:], ALU.is_equal, ALU.mult,
                                accum_out=rank[:, j:j + 1])
                            if j % 4 == 3:
                                ins.then_inc(source_used, 1)
                        dve.wait_ge(found, b + 2)
                        dve.tensor_tensor(picked[:], lp[:].rearrange("p (j n) -> p j n", n=LO),
                                          oh[u][:, q * BAT:(q + 1) * BAT, HI:HL], ALU.mult).then_inc(picked_ready, 1)
                        dve.wait_ge(picked_ready, b + 1)
                        dve.tensor_reduce(before[:], picked[:], AX.X, ALU.add).then_inc(before_ready, 1)
                        dve.wait_ge(before_ready, b + 1)
                        dve.wait_ge(source_used, 2 * b + 2 + 2)
                        dve.tensor_tensor(place[u][:, q * BAT:(q + 1) * BAT], before[:], rank[:], ALU.add)\
                            .then_inc(place_ready, 1)

        @block.scalar
        def _(act):
            act.sem_inc(found, 1)
            with act.Fori(0, NG * B3) as b:
                act.wait_ge(hi_turned, b + 1)
                act.wait_ge(found, b + 1)
                act.activation(hi_t[:], hp[0:HI, :].rearrange("p (j n) -> p j n", n=P), ACT.Copy).then_inc(hi_ready, 1)

        @block.tensor
        def _(pe):
            pe.wait_ge(ident_ready, 1)
            pe.sem_inc(source_used, 2)
            with pe.Fori(0, NG // 2) as i:
                for u in range(2):
                    g = 2 * i + u
                    pe.wait_ge(oh_ready, g + 1)
                    pe.wait_ge(src_ready, g + 1)
                    alone(pe, k)
                    for q in range(B3):
                        b = B3 * g + q
                        for j in range(BAT):
                            mm = pe.transpose(hp[0:HI, j * P:(j + 1) * P], oh[u][:, q * BAT + j, 0:HI], ident_b[:])
                        mm.then_inc(hi_turned, 1)
                        for j in range(BAT):
                            mm = pe.matmul(dp[0:HI, j * LO:(j + 1) * LO], oh[u][:, q * BAT + j, 0:HI],
                                           oh[u][:, q * BAT + j, HI:HL], start=True, stop=True, skip_group_check=True)
                        mm.then_inc(delta_ready, 1)
                        for j in range(BAT):
                            if j % 4 == 0:
                                pe.wait_ge(source_used, 2 * b + j // 4 + 1)
                            mm = pe.matmul(bp[j // 4][:, (j % 4) * P:(j % 4 + 1) * P],
                                           rows[u][:, q * BAT + j, EC:EC + 1].to_broadcast([P, P]), k.ident[:],
                                           start=True, stop=True, skip_group_check=True)
                            if j % 4 == 3:
                                mm.then_inc(source_ready, 1)
                        pe.wait_ge(hi_ready, b + 1)
                        pe.wait_ge(ring_ready, BAT * (b + 1))
                        for j in range(BAT):
                            mm = pe.matmul(lp[:, j * LO:(j + 1) * LO], hi_t[:, j, :], k.count_ring[u][:, q * BAT + j, :],
                                           start=True, stop=True, skip_group_check=True)
                        mm.then_inc(found, 1)


def scan(nc, k, d):
    R = 3
    W = 4 * P
    with ExitStack() as c:
        def sb(name, shape, dt=F32):
            return c.enter_context(nc.sbuf_tensor(name, shape, dt))

        def ps(name):
            return c.enter_context(nc.psum_tensor(name, [P, W], F32))

        def sem(name):
            return c.enter_context(nc.semaphore(name))
        rin = [sb(f"rin{r}", [P, QUARTERS, 4 * RW]) for r in range(R)]
        attr = [sb(f"attr{r}", [P, 4, QUARTERS * EC]) for r in range(R)]
        src_row = [sb(f"src_row{r}", [QUARTERS, W + 1]) for r in range(R)]
        flag_row = [sb(f"flag_row{r}", [QUARTERS, W], BF16) for r in range(R)]
        spread_b, same, bar = sb("spread_b", [QUARTERS, P], BF16), sb("same_src", [P, W]), sb("bar", [P, W])
        mx = [sb(f"mx{r}", [P, W]) for r in range(R)]
        sm = [sb(f"sm{r}", [P, W]) for r in range(R)]
        rout = [sb(f"rout{r}", [P, QUARTERS, 4, 2 * EC]) for r in range(R)]
        attr_ps = [ps(f"attr_ps{r}") for r in range(R)]
        srow_ps, flags_ps, mback, sback = ps("srow_ps"), ps("flags_ps"), ps("mback"), ps("sback")
        loaded = [sem(f"loaded{r}") for r in range(R)]
        stored = [sem(f"stored{r}") for r in range(R)]
        attr_copied, src_turned, src_copied = sem("attr_copied"), sem("src_turned"), sem("src_copied")
        flags_made, flags_spread, attr_turned = sem("flags_made"), sem("flags_spread"), sem("attr_turned")
        scanned, back_ready, back_copied, init, bar_ready = (
            sem("scanned"), sem("back_ready"), sem("back_copied"), sem("scan_init"), sem("bar_ready"))
        src_v = d.sorted.rearrange("(g s p k) c -> p s g (k c)", g=QUARTERS, s=STEPS, p=P)
        out_v = d.runs.rearrange("(g s p k) c -> p s g (k c)", g=QUARTERS, s=STEPS, p=P)
        LOOPS = STEPS // R
        block = c.enter_context(nc.Block())

        def in_steps(eng, step, peel=0):
            def at_step(i, q):
                def of(q, n):
                    return (i + q // R, q % R) if 0 <= n < STEPS else None
                n = R * i + q if isinstance(i, int) else R
                step(of(q + 2, n + 2), of(q + 1, n + 1), of(q, n))
            at_step(0, -2)
            at_step(0, -1)
            for q in range(R * peel):
                at_step(0, q)
            with eng.Fori(peel, LOOPS - 1) as i:
                for q in range(R):
                    at_step(i, q)
            for q in range(R):
                at_step(LOOPS - 1, q)

        @block.sync
        def _(sp):
            with sp.Fori(0, LOOPS) as i:
                for r in range(R):
                    n = R * i + r
                    sp.wait_ge(attr_copied, n + 1)
                    sp.wait_ge(src_turned, n + 1)
                    sp.dma_start(rin[r][:, None], src_v[:, bass.ds(n, 1)]).then_inc(loaded[r], 16)

        @block.gpsimd
        def _(pool):
            pool.sem_inc(attr_copied, R)
            with pool.Fori(0, LOOPS) as i:
                for r in range(R):
                    pool.wait_ge(attr_turned, R * i + r + 1)
                    pool.wait_ge(loaded[r], 16 * (i + 1))
                    alone(pool, k)
                    pool.tensor_copy(attr[r][:].rearrange("p k (g c) -> p g k c", c=EC),
                                     rin[r][:].rearrange("p g (k c) -> p g k c", c=RW)[:, :, :, 0:EC])\
                        .then_inc(attr_copied, 1)

        @block.tensor
        def _(pe):
            pe.sem_inc(src_turned, R)
            pe.sem_inc(attr_turned, R)
            pe.sem_inc(flags_spread, R)
            pe.sem_inc(back_ready, R)

            def step(a, b, c):
                if a:
                    (i, r), n = a, R * a[0] + a[1]
                    pe.wait_ge(loaded[r], 16 * (i + 1))
                    pe.wait_ge(src_copied, n + 1)
                    for q in range(4):
                        mm = pe.transpose(srow_ps[0:QUARTERS, q:W:4], rin[r][:, :, q * RW + EC], k.ident[:])
                    mm.then_inc(src_turned, 1)
                if b:
                    r, n = b[1], R * b[0] + b[1]
                    pe.wait_ge(flags_made, n + R + 1)
                    pe.wait_ge(bar_ready, n + 1)
                    pe.matmul(flags_ps[:], spread_b[:], flag_row[r][:], start=True, stop=True).then_inc(flags_spread, 1)
                    pe.wait_ge(attr_copied, n + R + 1)
                    pe.wait_ge(scanned, n + 1)
                    for q in range(4):
                        mm = pe.transpose(attr_ps[r][:, q:W:4], attr[r][:, q, :], k.ident[:])
                    mm.then_inc(attr_turned, 1)
                if c:
                    r, n = c[1], R * c[0] + c[1]
                    pe.wait_ge(scanned, n + R + 1)
                    pe.wait_ge(back_copied, n + 1)
                    for q in range(4):
                        pe.transpose(mback[:, q * P:(q + 1) * P], mx[r][:, q:W:4], k.ident[:])
                    for q in range(4):
                        mm = pe.transpose(sback[:, q * P:(q + 1) * P], sm[r][:, q:W:4], k.ident[:])
                    mm.then_inc(back_ready, 1)
            pe.wait_ge(init, 1)
            in_steps(pe, step)

        @block.scalar
        def _(act):
            act.sem_inc(src_copied, 1)
            act.sem_inc(back_copied, 1)
            act.sem_inc(bar_ready, 1)
            act.wait_ge(init, 1)

            def step(a, b, c):
                if a:
                    r, n = a[1], R * a[0] + a[1]
                    act.wait_ge(src_turned, n + R + 1)
                    act.wait_ge(flags_made, n + 1)
                    act.wait_ge(src_copied, n + 1)
                    act.activation(src_row[r][:, 0:1], src_row[(r - 1) % R][:, W:W + 1], ACT.Copy)
                    act.activation(src_row[r][:, 1:W + 1], srow_ps[0:QUARTERS, :], ACT.Copy).then_inc(src_copied, 1)
                if b:
                    n = R * b[0] + b[1]
                    act.wait_ge(flags_spread, n + R + 1)
                    act.wait_ge(scanned, n + R)
                    act.activation(same[:], flags_ps[:], ACT.Copy)
                    act.activation(bar[:], flags_ps[:], ACT.Copy, bias=-BIG, scale=BIG).then_inc(bar_ready, 1)
                if c:
                    (i, r), n = c, R * c[0] + c[1]
                    act.wait_ge(back_ready, n + R + 1)
                    if not isinstance(i, int) or i > 0:
                        act.wait_ge(stored[r], 16 * i)
                    act.activation(rout[r][:, :, :, 0:EC].rearrange("p g k c -> p k g c"),
                                   mback[:].rearrange("p (k g c) -> p k g c", k=4, c=EC), ACT.Copy)
                    act.activation(rout[r][:, :, :, EC:2 * EC].rearrange("p g k c -> p k g c"),
                                   sback[:].rearrange("p (k g c) -> p k g c", k=4, c=EC), ACT.Copy).then_inc(back_copied, 1)
                    act.wait_ge(back_copied, n + 2)
                    act.dma_start(out_v[:, bass.ds(n, 1)], rout[r][:].rearrange("p g k c -> p g (k c)")[:, None])\
                        .then_inc(stored[r], 16)
            in_steps(act, step, peel=1)
            for r in range(R):
                act.wait_ge(stored[r], 16 * LOOPS)

        @block.vector
        def _(dve):
            dve.tensor_copy(spread_b[:], k.spread[:])
            dve.memset(src_row[R - 1][:], -1.0)
            dve.memset(mx[R - 1][:], -BIG)
            dve.memset(sm[R - 1][:], 0.0).then_inc(init, 1)
            dve.wait_ge(init, 1)
            dve.sem_inc(scanned, R)
            dve.sem_inc(flags_made, R)

            def step(a, b, c):
                if a:
                    r, n = a[1], R * a[0] + a[1]
                    dve.wait_ge(src_copied, n + 2)
                    dve.wait_ge(flags_spread, n + 1)
                    dve.tensor_tensor(flag_row[r][:], src_row[r][:, 1:W + 1], src_row[r][:, 0:W], ALU.is_equal)\
                        .then_inc(flags_made, 1)
                if b:
                    r, n = b[1], R * b[0] + b[1]
                    dve.wait_ge(bar_ready, n + 2)
                    dve.wait_ge(attr_turned, n + R + 1)
                    dve.wait_ge(scanned, n + R)
                    dve.wait_ge(back_ready, n + 1)
                    dve.tensor_tensor_scan(mx[r][:], bar[:], attr_ps[r][:], mx[(r - 1) % R][:, W - 1:W], ALU.add, ALU.max)
                    dve.tensor_tensor_scan(sm[r][:], same[:], attr_ps[r][:], sm[(r - 1) % R][:, W - 1:W],
                                           ALU.mult, ALU.add).then_inc(scanned, 1)
            in_steps(dve, step)


def norm(dve, step, k, z, out, mean, var, var_ready, std_ready, at):
    sq = k.sq
    step(dve.tensor_reduce(mean[:], z[:], AX.X, ALU.add))
    step(dve.tensor_scalar(mean[:], mean[:], 1.0 / C, None, ALU.mult))
    step(dve.tensor_tensor(z[:], z[:], b3(mean[:], C), ALU.subtract))
    step(dve.tensor_tensor(sq[:], z[:], z[:], ALU.mult))
    step(dve.tensor_reduce(var[:], sq[:], AX.X, ALU.add))
    dve.tensor_scalar(var[:], var[:], 1.0 / C, EPS, ALU.mult, ALU.add).then_inc(var_ready, 1)
    dve.wait_ge(std_ready, at)
    step(dve.reciprocal(var[:], var[:]))
    return dve.tensor_tensor(out[:], z[:], b3(var[:], C), ALU.mult)


def nodes(nc, k, d):
    NF = 3 * EC + 2
    CH = [range(4 * c, min(4 * c + 4, NT)) for c in range((NT + 3) // 4)]
    with ExitStack() as c:
        def sb(name, shape, dt=F32):
            return c.enter_context(nc.sbuf_tensor(name, shape, dt))

        def ps(name):
            return c.enter_context(nc.psum_tensor(name, [P, 512], F32))

        def sem(name):
            return c.enter_context(nc.semaphore(name))
        at_f, at_i, end = sb("at_f", [P, NT]), sb("at_i", [P, NT], I32), sb("end_n", [P, NT])
        run = sb("run", [P, NT, 2 * EC])
        seam = sb("seam", [P, QUARTERS - 1, 2 * EC])
        cross, bar, some, per = sb("cross", [P, NT]), sb("bar_n", [P, NT]), sb("some", [P, NT]), sb("per", [P, NT])
        tmp, tmp_s, feat = sb("tmp_n", [P, NT, EC]), sb("tmp_s", [P, NT, EC]), sb("feat", [P, NT, NF])
        from_max, from_sum = sb("from_max", [P, NT, EC]), sb("from_sum", [P, NT, EC])
        ft = [sb(f"ft{b}", [NF, 512]) for b in range(2)]
        h1 = [sb(f"h1_{b}", [HID, 512]) for b in range(2)]
        z, mean, var = sb("z", [P, NT, C]), sb("mean", [P, NT]), sb("var", [P, NT])
        attr_mean = sb("attr_mean", [EC, 1])
        ft_ps, h1_ps = [ps(f"ft_ps{b}") for b in range(2)], [ps(f"h1_ps{b}") for b in range(2)]
        y_ps = ps("y_ps")
        t_ps = (ps("t_ps"), h1_ps[0])
        mean_ps, loop_ps = ps("mean_ps"), ps("loop_ps")
        at_ready, gathered, seam_in = sem("at_ready"), sem("gathered_n"), sem("seam_in")
        feat_ready, ft_turned, ft_ready, h1_done, h1_ready = sem("feat_ready"), sem("ft_turned"), sem("ft_ready"), sem("h1_done"), sem("h1_ready")
        y_done, y_used, dve_step, var_ready, std_ready = sem("y_done"), sem("y_used"), sem("nodes_dve"), sem("var_ready"), sem("std_ready")
        x_ready, x_turned, x_copied = sem("x_ready"), sem("x_turned"), sem("x_copied")
        sums_ready, mean_ready, attr_mean_ready, loop_ready = sem("sums_ready"), sem("mean_ready"), sem("attr_mean_ready"), sem("loop_ready")
        block = c.enter_context(nc.Block())

        @block.sync
        def _(sp):
            for g in range(QUARTERS - 1):
                row = (g + 1) * QROWS - 1
                sp.dma_start(seam[:, g, :], d.runs[row, :].partition_broadcast(P)).then_inc(seam_in, 16)

        @block.gpsimd
        def _(pool):
            pool.wait_ge(at_ready, 1)
            for i in range(NT):
                pool.indirect_dma_start(run[:, i, :], None, d.runs,
                                        bass.IndirectOffsetOnAxis(at_i[:, i:i + 1].bitcast(U32), 0)).then_inc(gathered, 16)

        @block.vector
        def _(dve):
            step = chain(dve, dve_step)
            step(dve.tensor_tensor(end[:], k.start_n[:], k.count_n[:], ALU.add))
            step(dve.tensor_scalar(at_f[:], end[:], -1.0, 0.0, ALU.add, ALU.max))
            dve.tensor_copy(at_i[:], at_f[:]).then_inc(at_ready, 1)
            dve.wait_ge(seam_in, 16 * (QUARTERS - 1))
            for g in range(QUARTERS - 1):
                row = float((g + 1) * QROWS)
                step(dve.tensor_scalar(cross[:], k.start_n[:], row, None, ALU.is_lt))
                step(dve.scalar_tensor_tensor(cross[:], end[:], row, cross[:], ALU.is_gt, ALU.mult))
                step(dve.tensor_scalar(bar[:], cross[:], -1.0, BIG, ALU.add, ALU.mult))
                to_max, to_sum = (tmp, tmp_s) if g else (from_max, from_sum)
                dve.tensor_tensor(to_max[:], rep(seam[:, g, 0:EC], NT), b3(bar[:], EC), ALU.add)
                step(dve.tensor_tensor(to_sum[:], rep(seam[:, g, EC:2 * EC], NT), b3(cross[:], EC), ALU.mult))
                if g:
                    dve.tensor_tensor(from_max[:], from_max[:], tmp[:], ALU.max)
                    step(dve.tensor_tensor(from_sum[:], from_sum[:], tmp_s[:], ALU.add))
            dve.wait_ge(gathered, 16 * NT)
            dve.tensor_tensor(run[:, :, 0:EC], run[:, :, 0:EC], from_max[:], ALU.max)
            step(dve.tensor_tensor(run[:, :, EC:2 * EC], run[:, :, EC:2 * EC], from_sum[:], ALU.add))
            dve.tensor_scalar(some[:], k.count_n[:], 0.0, None, ALU.is_gt)
            step(dve.tensor_scalar(per[:], k.count_n[:], 1.0, None, ALU.max))
            dve.tensor_tensor(feat[:, :, 0:EC], run[:, :, EC:2 * EC], b3(some[:], EC), ALU.mult)
            dve.tensor_tensor(feat[:, :, EC:2 * EC], run[:, :, 0:EC], b3(some[:], EC), ALU.mult)
            step(dve.reciprocal(per[:], per[:]))
            dve.tensor_copy(feat[:, :, 3 * EC:3 * EC + 1], k.u[:, 0:1].to_broadcast([P, NT])[:, :, None])
            dve.memset(feat[:, :, 3 * EC + 1:NF], 1.0)
            dve.tensor_tensor(feat[:, :, 2 * EC:3 * EC], feat[:, :, 0:EC], b3(per[:], EC), ALU.mult).then_inc(feat_ready, 1)
            dve.tensor_tensor(k.x[:], k.x[:], rep(k.b2[:], NT), ALU.add).then_inc(x_ready, 1)
            dve.wait_ge(x_ready, 1)
            for n, tiles in enumerate(CH):
                w = len(tiles)
                dve.wait_ge(y_done, n + 1)
                dve.tensor_tensor(z[:, tiles[0]:tiles[0] + w, :], k.x[:, tiles[0]:tiles[0] + w, :],
                                  y_ps[:, 0:w * C].rearrange("p (i n) -> p i n", n=C), ALU.add).then_inc(y_used, 1)
            dve.wait_ge(y_used, len(CH))
            norm(dve, step, k, z, k.x, mean, var, var_ready, std_ready, 1).then_inc(x_ready, 1)
            dve.wait_ge(sums_ready, 1)
            dve.tensor_scalar(attr_mean[:], mean_ps[0:EC, 0:1], 1.0 / EDGES, None, ALU.mult).then_inc(attr_mean_ready, 1)
            dve.wait_ge(loop_ready, 1)
            dve.tensor_copy(k.loop_all[:], loop_ps[:, 0:LAYERS * C].rearrange("p (l n) -> p l n", l=LAYERS))

        @block.scalar
        def _(act):
            def copy_features(n):
                w = len(CH[n]) * P
                act.wait_ge(ft_turned, n + 1)
                if n >= 2:
                    act.wait_ge(h1_done, n - 1)
                act.activation(ft[n % 2][:, 0:w], ft_ps[n % 2][0:NF, 0:w], ACT.Copy).then_inc(ft_ready, 1)

            copy_features(0)
            for n, tiles in enumerate(CH):
                w = len(tiles) * P
                if n + 1 < len(CH):
                    copy_features(n + 1)
                act.wait_ge(h1_done, n + 1)
                if n >= 2:
                    act.wait_ge(y_done, n - 1)
                act.activation(h1[n % 2][:, 0:w], h1_ps[n % 2][:, 0:w], ACT.Relu).then_inc(h1_ready, 1)
            act.wait_ge(var_ready, 1)
            act.activation(var[:], var[:], ACT.Sqrt).then_inc(std_ready, 1)
            for n, tiles in enumerate(CH):
                w = len(tiles) * P
                act.wait_ge(x_turned, n + 1)
                act.activation(k.hT[0:C, tiles[0] * P:tiles[0] * P + w], t_ps[n % 2][0:C, 0:w], ACT.Copy).then_inc(x_copied, 1)

        @block.tensor
        def _(pe):
            pe.wait_ge(feat_ready, 1)
            def turn_features(n):
                if n >= 2:
                    pe.wait_ge(ft_ready, n - 1)
                for j, i in enumerate(CH[n]):
                    mm = pe.transpose(ft_ps[n % 2][0:NF, j * P:(j + 1) * P], feat[:, i, :], k.ident[:])
                mm.then_inc(ft_turned, 1)

            def hidden(n):
                w = len(CH[n]) * P
                if n >= 2:
                    pe.wait_ge(h1_ready, n - 1)
                pe.wait_ge(ft_ready, n + 1)
                pe.matmul(h1_ps[n % 2][:, 0:w], k.w1[:], ft[n % 2][:, 0:w], start=True, stop=True).then_inc(h1_done, 1)

            turn_features(0)
            turn_features(1)
            hidden(0)
            for n, tiles in enumerate(CH):
                w = len(tiles)
                if n + 2 < len(CH):
                    turn_features(n + 2)
                if n + 1 < len(CH):
                    hidden(n + 1)
                if n:
                    pe.wait_ge(y_used, n)
                pe.wait_ge(h1_ready, n + 1)
                for j in range(w):
                    mm = pe.matmul(y_ps[:, j * C:(j + 1) * C], h1[n % 2][:, j * P:(j + 1) * P], k.w2[:],
                                   start=True, stop=True, skip_group_check=True)
                mm.then_inc(y_done, 1)
            for i in range(NT):
                mm = pe.matmul(mean_ps[0:EC, 0:1], feat[:, i, 0:EC], k.ones[:, 0:1], start=(i == 0), stop=(i == NT - 1))
            mm.then_inc(sums_ready, 1)
            pe.wait_ge(x_ready, 2)
            for n, tiles in enumerate(CH):
                if n >= 2:
                    pe.wait_ge(x_copied, n - 1)
                for j, i in enumerate(tiles):
                    mm = pe.transpose(t_ps[n % 2][0:C, j * P:(j + 1) * P], k.x[:, i, :], k.ident[:])
                mm.then_inc(x_turned, 1)
            pe.wait_ge(attr_mean_ready, 1)
            pe.matmul(loop_ps[:, 0:LAYERS * C], attr_mean[:].to_broadcast([EC, P]), k.wc[:],
                      start=True, stop=True).then_inc(loop_ready, 1)


def finish(nc, k, d, s, l):
    CH = [range(4 * n, min(4 * n + 4, NT)) for n in range((NT + 3) // 4)]
    N = len(CH)
    PART = [slice(0, 12), slice(12, NT)]
    with ExitStack() as c:
        def sb(name, shape, dt=F32):
            return c.enter_context(nc.sbuf_tensor(name, shape, dt))
        fp = [c.enter_context(nc.psum_tensor(f"fin_ps{b}", [P, 512], F32)) for b in range(2)]
        tp = [c.enter_context(nc.psum_tensor(f"hT_ps{b}", [P, 512], F32)) for b in range(4)]
        sums, el = sb("sums", [P, NT, SC]), sb("el", [P, NT, C])
        top = sb("top", [P, NT])
        w2, den = sb("w_pair", [P, 2, NT]), sb("den", [P, NT])
        block = c.enter_context(nc.Block())
        STEPS_F = 9

        @block.tensor
        def _(pe):
            for n, tiles in enumerate(CH):
                if n >= 2:
                    if n % 2:
                        pe.wait_ge(s.sums_copied_a, N // 2 * l + n // 2)
                    else:
                        pe.wait_ge(s.sums_copied, (N - N // 2) * l + n // 2)
                for j, i in enumerate(tiles):
                    mm = pe.transpose(fp[n % 2][:, j * SC:(j + 1) * SC], k.acc[0:SC, i * P:(i + 1) * P], k.ident[0:SC, 0:SC])
                mm.then_inc(s.sums_turned, 1)
            for n, tiles in enumerate(CH):
                if n in (0, 3):
                    pe.wait_ge(s.h_ready, 2 * l + n // 3 + 1)
                if n >= 4:
                    pe.wait_ge(s.h_copied, 5 * l + n - 3)
                if n in (0, 3) or n >= 4:
                    alone(pe, k)
                for j, i in enumerate(tiles):
                    mm = pe.transpose(tp[n % 4][0:C, j * P:(j + 1) * P], k.h[:, i, :], k.ident[:])
                mm.then_inc(s.h_turned, 1)

        @block.scalar
        def _(act):
            for n, tiles in enumerate(CH):
                if n % 2:
                    w = len(tiles)
                    act.wait_ge(s.sums_turned, N * l + n + 1)
                    act.activation(sums[:, tiles[0]:tiles[0] + w, :],
                                   fp[1][:, 0:w * SC].rearrange("p (i n) -> p i n", n=SC), ACT.Copy).then_inc(s.sums_copied_a, 1)
            act.wait_ge(s.pair_ready, l + 1)
            act.activation(w2[:], w2[:], ACT.Exp).then_inc(s.pair_exp, 1)
            for n, tiles in enumerate(CH):
                if n < 3 or n % 2 == 0:
                    w = len(tiles) * P
                    act.wait_ge(s.h_turned, N * l + n + 1)
                    act.activation(k.hT[0:C, tiles[0] * P:tiles[0] * P + w], tp[n % 4][0:C, 0:w], ACT.Relu,
                                   bias=k.bias_c[:, 0:1]).then_inc(s.h_copied, 1)

        @block.vector
        def _(dve):
            done = [0]

            def step(ins):
                done[0] += 1
                ins.then_inc(s.finish_step, 1)
                dve.wait_ge(s.finish_step, STEPS_F * l + done[0])
            for n, tiles in enumerate(CH):
                if n % 2 == 0:
                    w = len(tiles)
                    dve.wait_ge(s.sums_turned, N * l + n + 1)
                    dve.tensor_copy(sums[:, tiles[0]:tiles[0] + w, :],
                                    fp[0][:, 0:w * SC].rearrange("p (i n) -> p i n", n=SC)).then_inc(s.sums_copied, 1)
            dve.wait_ge(s.sums_copied, (N - N // 2) * (l + 1))
            dve.wait_ge(s.sums_copied_a, N // 2 * (l + 1))
            shift = sums[:, :, SC - 1]
            step(dve.tensor_tensor(top[:], shift, k.loop_score[:], ALU.max))
            dve.tensor_tensor(w2[:, 0, :], shift, top[:], ALU.subtract)
            dve.tensor_tensor(w2[:, 1, :], k.loop_score[:], top[:], ALU.subtract).then_inc(s.pair_ready, 1)
            dve.wait_ge(s.pair_exp, l + 1)
            step(dve.tensor_tensor(den[:], sums[:, :, C], w2[:, 0, :], ALU.mult))
            step(dve.scalar_tensor_tensor(den[:], den[:], DEN_EPS, w2[:, 1, :], ALU.add, ALU.add))
            step(dve.reciprocal(den[:], den[:]))
            step(dve.tensor_tensor(w2[:], w2[:], den[:, None, :].to_broadcast([P, 2, NT]), ALU.mult))
            for t in PART:
                dve.tensor_tensor(k.h[:, t, :], sums[:, t, 0:C], b3(w2[:, 0, t], C), ALU.mult)
                step(dve.tensor_tensor(el[:, t, :], k.xlr[:, t, 0:C], b3(w2[:, 1, t], C), ALU.mult))
                step(dve.tensor_tensor(k.h[:, t, :], k.h[:, t, :], el[:, t, :], ALU.add))
                dve.sem_inc(s.h_ready, 1)
            for n, tiles in enumerate(CH):
                if n >= 3 and n % 2:
                    w = len(tiles) * P
                    dve.wait_ge(s.h_turned, N * l + n + 1)
                    dve.tensor_scalar(k.hT[0:C, tiles[0] * P:tiles[0] * P + w], tp[n % 4][0:C, 0:w], k.bias_c[:, 0:1],
                                      0.0, ALU.add, ALU.max).then_inc(s.h_copied_v, 1)
            assert done[0] == STEPS_F


def output(nc, k, d):
    with ExitStack() as c:
        mean, var = (c.enter_context(nc.sbuf_tensor(n, [P, NT], F32)) for n in ("mean_o", "var_o"))
        dve_step, var_ready, std_ready, z_ready, out_done = (
            c.enter_context(nc.semaphore(n)) for n in ("out_dve", "var_o_ready", "std_o_ready", "z_ready", "out_done"))
        block = c.enter_context(nc.Block())
        full = NODES // P

        @block.vector
        def _(dve):
            step = chain(dve, dve_step)
            step(dve.tensor_tensor(k.x[:], k.x[:], k.h[:], ALU.add))
            step(dve.tensor_tensor(k.x[:], k.x[:], rep(k.bias[:], NT), ALU.add))
            norm(dve, step, k, k.x, k.h, mean, var, var_ready, std_ready, 1).then_inc(z_ready, 1)

        @block.scalar
        def _(act):
            act.wait_ge(var_ready, 1)
            act.activation(var[:], var[:], ACT.Sqrt).then_inc(std_ready, 1)

        @block.sync
        def _(sp):
            sp.wait_ge(z_ready, 1)
            sp.dma_start(d.out[0:full * P, :].rearrange("(i p) n -> p i n", p=P), k.h[:, 0:full, :]).then_inc(out_done, 16)
            sp.dma_start(d.out[full * P:NODES, :], k.h[0:NODES - full * P, full, :]).then_inc(out_done, 16)
            sp.wait_ge(out_done, 32)


def edges(nc, k, d, s, l):
    R = 3
    SLOT = [(NG - r + R - 1) // R for r in range(R)]
    HALF = G // 2
    PAD = T - (EDGES + P - 1) // P
    NB = G // 4
    with ExitStack() as c:
        def sb(name, shape, dt=F32):
            return c.enter_context(nc.sbuf_tensor(name, shape, dt))

        def ps(name):
            return c.enter_context(nc.psum_tensor(name, [P, 512], F32))
        m = [sb(f"m{r}", [P, G, P]) for r in range(R)]
        mt = sb("mt", [P, G, P])
        xg = [sb(f"xg{r}", [P, G, C]) for r in range(R)]
        idx = [sb(f"idx{r}", [P, G], I32) for r in range(R)]
        xw = [sb(f"xw{r}", [P, G, C]) for r in range(R)]
        at = [sb(f"at{r}", [P, G // 4 * P]) for r in range(R)]
        ids = [sb(f"ids_e{r}", [G, P], I32) for r in range(R)]
        e = k.h[:, 0:G, :]
        score = [sb(f"score{r}", [P, G]) for r in range(R)]
        bar, last, first, run = sb("bar_e", [G, P]), sb("last", [G, P]), sb("first", [G, P]), sb("run_e", [G, P])
        ends, shift = sb("ends", [G, P]), sb("shift", [G, P])
        dif, wt, shift_out = sb("dif", [G, P + 1]), sb("wt", [G, P + 1]), sb("shift_out", [G, P])
        crow, cin_row, cin = sb("crow", [1, G + 1]), sb("cin_row", [1, G]), sb("cin", [G, 1])
        scale_d = sb("scale_d", [G, G])
        sw = [sb(f"sw{r}", [P, G, SC]) for r in range(R)]
        in_last = [sb(f"in_last{r}", [P, G]) for r in range(R)]
        keep, carried = sb("keep", [SC, G]), sb("carried", [SC, G])
        m_ps = [ps(f"m_ps{b}") for b in range(2)]
        e_ps = [ps(f"e_ps{b}") for b in range(2)]
        agg_ps = [ps(f"agg_ps{b}") for b in range(2)]
        s_ps, w_ps = ps("s_ps"), ps("w_ps")
        st = s_ps[0:G, 0:P]
        cin_ps = s_ps[0:G, P:P + 1]
        res_ps, tail_ps = s_ps[0:SC, 256:256 + G], s_ps[0:SC, 320:320 + G]
        top_row = w_ps[0:1, 0:G]
        wt_ps, sh_ps = w_ps[:, 32:32 + G], w_ps[:, 64:64 + G]
        block = c.enter_context(nc.Block())
        CH = [range(t, min(t + 4, NT)) for t in range(0, NT, 4)]
        N_CH = len(CH)

        def copied(eng, n):
            if n % 2:
                eng.wait_ge(s.rows_ready_a, N_CH // 2 * l + n // 2 + 1)
            else:
                eng.wait_ge(s.rows_ready_v, (N_CH - N_CH // 2) * l + n // 2 + 1)

        def rows_of_chunk(n):
            tiles = CH[n]
            return (k.xlr[:, tiles[0]:tiles[-1] + 1, :],
                    e_ps[n % 2][:, 0:len(tiles) * P].rearrange("p (j n) -> p j n", n=2 * C))

        def norm_i(i, q):
            return i + q // R, q % R

        def gathers(i, r):
            return G - PAD if isinstance(i, int) and i * R + r == NG - 1 else G

        def done_with(eng, of, q, tiles, *sems):
            if skipped(of, q + 1, tiles) and not skipped(of, q, tiles):
                for sem, per in sems:
                    eng.sem_inc(sem, (G // tiles - 1 - q) * per)

        def skipped(of, q, tiles):
            return q < G // tiles and q * tiles >= gathers(*of)

        def N(i, r):
            return l * NG + i * R + r

        def nth(i, r):
            return l * SLOT[r] + i

        def in_order(eng, one, peel=0):
            one(0, 0)
            with eng.Fori(0, (NG - 1) // R - peel) as i:
                for q in range(1, R + 1):
                    one(*norm_i(i, q))
            for q in range(1, R * peel + 1):
                one(*norm_i((NG - 1) // R - peel, q))

        def in_steps(eng, step):
            def at_step(i, q):
                def of(q, g):
                    return norm_i(i, q) if 0 <= g < NG else None
                g = R * i + q if isinstance(i, int) else R
                step(of(q + 2, g + 2), of(q + 1, g + 1), of(q, g), of(q - 1, g - 1))
            full = (NG - 2 - 1) // R
            at_step(0, -1)
            at_step(0, 0)
            with eng.Fori(0, full) as i:
                for q in range(1, R + 1):
                    at_step(i, q)
            for g in range(R * full + 1, NG + 1):
                at_step(full, g - R * full)

        @block.sync
        def _(sp):
            def sources(i, r):
                sp.wait_ge(s.score_ready, N(i, r) + 1)
                sp.dma_start(idx[r][:], d.src[:, bass.ds((i * R + r) * G, G)]).then_inc(s.idx_in[r], 16)

            def load(i, r):
                g = i * R + r
                if not isinstance(i, int) or g + 1 < NG:
                    sources(*norm_i(i, r + 1))
                for h in range(2):
                    _, base = nc.values_load_multi_w_load_instructions(
                        k.base_i[0:1, bass.ds(g * G + h * HALF, HALF)], engines=[ENG.SP], min_val=0, max_val=NODES,
                        skip_runtime_bounds_check_because=WIN)
                    if h == 0:
                        sp.wait_ge(s.e_ready, N(i, r) * 3 + 3)
                        sp.dma_start(at[r][:], d.attrt[:, bass.ds(g * (G // 4 * P), G // 4 * P)]).then_inc(s.at_in[r], 16)
                        sp.wait_ge(s.weighted, N(i, r) + 1)
                        sp.dma_start(ids[r][:], d.dstg[:, bass.ds(g * P, P)]).then_inc(s.ids_in[r], 16)
                    for j in range(HALF):
                        sp.dma_start(xw[r][:, h * HALF + j, :], d.xr_d[bass.ds(base[j], P), :]).then_inc(s.xw_in[r], 16)
            sources(0, 0)
            for n, tiles in enumerate(CH):
                copied(sp, n)
                t = slice(tiles[0], tiles[-1] + 1)
                sp.dma_start(d.xl_d.rearrange("(i p) n -> p i n", p=P)[:, t, :], k.xlr[:, t, 0:C]).then_inc(s.xl_out, 16)
            for part in (slice(0, NT // 2), slice(NT // 2, NT)):
                sp.dma_start(d.xr_d[0:NPAD, :].rearrange("(i p) n -> p i n", p=P)[:, part, :],
                             k.xlr[:, part, C:2 * C]).then_inc(s.xr_out, 16)
            sp.wait_ge(s.xr_out, 32 * (l + 1))
            alone(sp, k)
            in_order(sp, load, peel=1)

        @block.gpsimd
        def _(pool):
            def gather(i, r):
                pool.wait_ge(s.weighted, N(i, r) + 1)
                pool.wait_ge(s.idx_in[r], (nth(i, r) + 1) * 16)
                alone(pool, k)
                for j in range(gathers(i, r)):
                    pool.indirect_dma_start(xg[r][:, j, :], None, d.xl_d,
                                            bass.IndirectOffsetOnAxis(idx[r][:, j:j + 1].bitcast(U32), 0))\
                        .then_inc(s.gathered[r], 16)
            pool.wait_ge(s.xl_out, 16 * N_CH * (l + 1))
            alone(pool, k)
            in_order(pool, gather, peel=1)

        @block.vector
        def _(dve):
            def one_hot(i, r):
                dve.wait_ge(s.agg_ready, N(i, r) * NB + 2)
                dve.tensor_tensor(m[r][:], rep(k.iota[:], G), b3(k.loc[:, bass.ds((i * R + r) * G, G)], P), ALU.is_equal)\
                    .then_inc(s.m_ready, 1)

            def loops():
                done = [0]

                def step(ins):
                    done[0] += 1
                    ins.then_inc(s.loop_step, 1)
                    dve.wait_ge(s.loop_step, l * 5 + done[0])
                copied(dve, N_CH - 2)
                copied(dve, N_CH - 1)
                step(dve.tensor_tensor(k.h[:], k.xlr[:, :, 0:C], k.xlr[:, :, C:2 * C], ALU.add))
                step(dve.tensor_tensor(k.h[:], k.h[:], rep(k.loop[:], NT), ALU.add))
                step(dve.scalar_tensor_tensor(k.h[:], k.h[:], NEG_SLOPE, k.h[:], ALU.mult, ALU.max))
                step(dve.tensor_tensor(k.h[:], k.h[:], rep(k.att[:], NT), ALU.mult))
                step(dve.tensor_reduce(k.loop_score[:], k.h[:], AX.X, ALU.add))

            def add(q, i, r):
                if skipped((i, r), q, BAT):
                    return
                if q == 0:
                    of_slot = SLOT[r] * G - (PAD if r == (NG - 1) % R else 0)
                    dve.wait_ge(s.gathered[r], l * (16 * of_slot) + i * (16 * G) + 16 * gathers(i, r))
                dve.wait_ge(s.e_ready, N(i, r) * 3 + q + 1 + 9)
                dve.tensor_tensor(e[:, q * BAT:(q + 1) * BAT, :], e_ps[q % 2][:].rearrange("p (j n) -> p j n", n=C),
                                  xg[r][:, q * BAT:(q + 1) * BAT, :], ALU.add).then_inc(s.e_used, 1)
                done_with(dve, (i, r), q, BAT, (s.e_ready, 1))

            def scores(i, r):
                n = N(i, r)
                done = sum(not skipped((i, r), q, BAT) for q in range(3))
                dve.wait_ge(s.e_used, n * 3 + done + 2)
                if done < 3:
                    dve.sem_inc(s.e_used, 3 - done)
                dve.scalar_tensor_tensor(e[:], e[:], NEG_SLOPE, e[:], ALU.mult, ALU.max).then_inc(s.e_step, 1)
                dve.wait_ge(s.e_step, n * 2 + 1)
                dve.tensor_tensor(e[:], e[:], rep(k.att[:], G), ALU.mult).then_inc(s.e_step, 1)
                dve.wait_ge(s.e_step, n * 2 + 2)
                dve.tensor_reduce(score[r][:], e[:], AX.X, ALU.add).then_inc(s.score_ready, 1)

            def weights(i, r):
                g, n = i * R + r, N(i, r)
                done = [0]

                def step(ins):
                    done[0] += 1
                    ins.then_inc(s.b_step, 1)
                    dve.wait_ge(s.b_step, n * 12 + done[0])
                dve.wait_ge(s.ids_in[r], (nth(i, r) + 1) * 16)
                step(dve.tensor_tensor(k.eq[:, 1:P], ids[r][:, 1:P], ids[r][:, 0:P - 1], ALU.is_equal))
                dve.tensor_scalar(bar[:], k.eq[:, 0:P], -1.0, BIG, ALU.add, ALU.mult)
                dve.tensor_scalar(last[:], k.eq[:, 1:P + 1], -1.0, 1.0, ALU.mult, ALU.add)
                dve.tensor_copy(cin[:], ids[r][:, 0:1]).then_inc(s.first_id, 1)
                dve.wait_ge(s.first_id, n + 1)
                step(dve.tensor_scalar(first[:], ids[r][:], cin[:, 0:1], -1.0, ALU.is_equal, ALU.add))
                dve.tensor_copy(in_last[r][:], k.in_last[:, bass.ds(g * G, G)])
                dve.wait_ge(s.scores_turned, n + 1)
                dve.tensor_tensor_scan(run[:], bar[:], st, -BIG, ALU.add, ALU.max).then_inc(s.run_ready, 1)
                step(dve.tensor_copy(crow[:, 0:1], k.carry[:]))
                dve.wait_ge(s.top_turned, n + 1)
                step(dve.tensor_tensor_scan(crow[:, 1:G + 1], k.carry_b[:, bass.ds(g * G, G)], top_row, k.carry[:, 0:1],
                                            ALU.add, ALU.max))
                dve.tensor_tensor(cin_row[:], crow[:, 0:G], k.cont_b[:, bass.ds(g * G, G)], ALU.add).then_inc(s.cin_row_ready, 1)
                dve.tensor_copy(k.carry[:], crow[:, G:G + 1])
                step(dve.tensor_tensor(ends[:], run[:], last[:], ALU.mult))
                step(dve.tensor_tensor_scan(shift[:, ::-1], k.eq[:, 1:P + 1][:, ::-1], ends[:, ::-1], 0.0, ALU.mult, ALU.add))
                dve.wait_ge(s.cin_turned, n + 1)
                step(dve.tensor_copy(cin[:], cin_ps))
                step(dve.tensor_scalar(first[:], first[:], BIG, cin[:, 0:1], ALU.mult, ALU.add))
                step(dve.tensor_tensor(shift[:], shift[:], first[:], ALU.max))
                dve.tensor_tensor(dif[:, P:P + 1], cin[:], shift[:, 0:1], ALU.subtract)
                dve.tensor_tensor(dif[:, 0:P], st, shift[:], ALU.subtract).then_inc(s.dif_ready, 1)
                step(dve.tensor_tensor(shift_out[:], shift[:], last[:], ALU.mult))
                dve.wait_ge(s.weights_done, n + 1)
                dve.tensor_scalar(scale_d[:], k.ident[0:G, 0:G], wt[:, P:P + 1], None, ALU.mult).then_inc(s.scale_ready, 1)
                dve.wait_ge(s.weights_turned, n + 1)
                dve.wait_ge(s.agg_ready, n * NB + 2)
                step(dve.tensor_copy(sw[r][:, :, C:SC], w_ps[:, 32:96].rearrange("p (a j) -> p j a", a=2)[:, 0:G, :]))
                step(dve.tensor_tensor(sw[r][:, :, 0:C], xg[r][:], b3(sw[r][:, :, C], C), ALU.mult))
                assert done[0] == 12
                dve.sem_inc(s.weighted, 1)

            def carry(i, r):
                g, n = i * R + r, N(i, r)
                done = [0]

                def step(ins):
                    done[0] += 1
                    ins.then_inc(s.c_step, 1)
                    dve.wait_ge(s.c_step, n * 3 + done[0])
                dve.wait_ge(s.tails_ready, n + 1)
                step(dve.tensor_tensor(keep[:], k.single[:, bass.ds(g * G, G)], res_ps, ALU.mult))
                step(dve.tensor_tensor_scan(k.partial[:, 1:G + 1], keep[:], tail_ps, k.partial[:, 0:1], ALU.mult, ALU.add))
                dve.wait_ge(s.agg_ready, n * NB + 14)
                step(dve.tensor_tensor(carried[:], k.partial[:, 0:G], res_ps, ALU.mult))
                dve.tensor_copy(k.partial[:, 0:1], k.partial[:, G:G + 1]).then_inc(s.carried_ready, 1)
                dve.wait_ge(s.carried_ready, n + 1)

            def step(mg, a, b, c):
                if b:
                    weights(*b)
                elif mg:
                    one_hot(0, 0)
                    one_hot(*mg)
                    loops()
                if a:
                    add(0, *a)
                    add(1, *a)
                if a:
                    add(2, *a)
                    scores(*a)
                if b:
                    carry(*b)
                if mg and b:
                    one_hot(*mg)
            dve.tensor_copy(k.wlr[:], k.wlr_all[:, bass.ds(l, 1), :].rearrange("p a n -> p (a n)")).then_inc(s.weights_ready, 1)
            for to, of in ((k.att, k.att_all), (k.bias, k.bias_all), (k.loop, k.loop_all), (k.bd, k.bd_all)):
                dve.tensor_copy(to[:], of[:, bass.ds(l, 1), :].rearrange("p a n -> p (a n)"))
            dve.tensor_copy(k.bias_c[:], k.biast[:, bass.ds(l, 1)])
            for n in range(0, N_CH, 2):
                dve.wait_ge(s.projected, N_CH * l + n + 1)
                dve.tensor_copy(*rows_of_chunk(n)).then_inc(s.rows_ready_v, 1)
            in_steps(dve, step)
            alone(dve, k)

        @block.scalar
        def _(act):
            base = []

            def step(mg, a, b, c):

                def evacuate(q):
                    if not a or skipped(a, q, 4):
                        return
                    n = N(*a)
                    if q % 2 == 0:
                        act.wait_ge(s.e_ready, n * 3 + q // 2 + 7)
                    act.wait_ge(s.m_turned, n * NB + q + 1)
                    act.activation(mt[:, 4 * q:4 * q + 4, :], m_ps[q % 2][:].rearrange("p (j n) -> p j n", n=P), ACT.Copy)\
                        .then_inc(s.m_evacuated, 1)
                    done_with(act, a, q, 4, (s.m_turned, 1))

                def place(q):
                    if not c or skipped(c, q, 4):
                        return
                    n, g = N(*c), c[0] * R + c[1]
                    if q % 3 == 0:
                        base[:] = nc.values_load_multi_w_load_instructions(
                            k.base_i[0:1, bass.ds(g * G + q * 4, HALF)], engines=[ENG.Activation], min_val=0,
                            max_val=NODES, skip_runtime_bounds_check_because=WIN)[1]
                    act.wait_ge(s.agg_ready, n * NB + q + 1 + 14)
                    for j in range(4):
                        act.wait_ge(s.window_done, n * G + 4 * q + j + 1)
                        alone(act, k)
                        act.activation(k.acc[0:SC, bass.ds(base[4 * (q % 3) + j], P)],
                                       agg_ps[q % 2][0:SC, j * P:(j + 1) * P], ACT.Copy).then_inc(s.window_done, 1)
                    act.wait_ge(s.window_done, n * G + 4 * q + 5)
                    act.sem_inc(s.agg_evacuated, 1)
                    done_with(act, c, q, 4, (s.agg_ready, 1), (s.agg_evacuated, 1), (s.window_done, 4))

                place(0)
                evacuate(0)
                evacuate(1)
                evacuate(2)
                if not a:
                    place(1)
                if b:
                    act.wait_ge(s.dif_ready, N(*b) + 1)
                    act.activation(wt[:], dif[:], ACT.Exp).then_inc(s.weights_done, 1)
                evacuate(3)
                if a:
                    place(1)
                evacuate(4)
                place(2)
                evacuate(5)
                for q in range(3, NB):
                    place(q)
            for n in range(1, N_CH, 2):
                act.wait_ge(s.projected, N_CH * l + n + 1)
                to, of = rows_of_chunk(n)
                act.activation(to, of, ACT.Copy).then_inc(s.rows_ready_a, 1)
            in_steps(act, step)

        @block.tensor
        def _(pe):
            pe.wait_ge(s.weights_ready, l + 1)
            for n, tiles in enumerate(CH):
                if n >= 2:
                    copied(pe, n - 2)
                for j, i in enumerate(tiles):
                    mm = pe.matmul(e_ps[n % 2][:, j * P:(j + 1) * P], k.hT[0:C + 1, i * P:(i + 1) * P], k.wlr[:],
                                   start=True, stop=True, skip_group_check=True)
                mm.then_inc(s.projected, 1)

            def step(mg, a, b, c):
                if b:
                    nb, rb = N(*b), b[1]

                def turn(q):
                    if not a or skipped(a, q, 4):
                        return
                    n, r = N(*a), a[1]
                    if q == 0:
                        pe.wait_ge(s.m_ready, n + 1)
                    pe.wait_ge(s.m_evacuated, n * NB + q + 1)
                    for j in range(4):
                        mm = pe.transpose(m_ps[q % 2][:, j * P:(j + 1) * P], m[r][:, 4 * q + j, :], k.ident[:])
                    mm.then_inc(s.m_turned, 1)

                def add_up(q):
                    if not a or skipped(a, q, BAT):
                        return
                    n, r = N(*a), a[1]
                    if q == 0:
                        pe.wait_ge(s.at_in[r], (nth(*a) + 1) * 16)
                        pe.wait_ge(s.xw_in[r], (nth(*a) + 1) * (16 * G))
                    pe.wait_ge(s.e_used, n * 3 + (2, 1, 3)[q])
                    pe.wait_ge(s.m_evacuated, n * NB + 2 * q + 4)
                    out = e_ps[q % 2]
                    for h in range(2):
                        t = (2 * q + h) * P
                        pe.matmul(out[:, h * 256:(h + 1) * 256], at[r][:, t:t + P], k.bd[:], start=(h == 0), stop=False,
                                  skip_group_check=True)
                    for j in range(BAT):
                        mm = pe.matmul(out[:, j * C:(j + 1) * C], mt[:, q * BAT + j, :], xw[r][:, q * BAT + j, :],
                                       start=False, stop=(j == BAT - 1), skip_group_check=True)
                    mm.then_inc(s.e_ready, 1)
                    done_with(pe, a, q, BAT, (s.m_evacuated, 2))

                def sum_up(q):
                    if not c or skipped(c, q, 4):
                        return
                    n, r = N(*c), c[1]
                    pe.wait_ge(s.agg_evacuated, n * NB + q + 1)
                    out = agg_ps[q % 2]
                    for j in range(4):
                        pe.matmul(out[0:SC, j * P:(j + 1) * P], sw[r][:, 4 * q + j, :], m[r][:, 4 * q + j, :],
                                  start=(j == 0), stop=False, skip_group_check=True)
                    pe.matmul(out[0:SC, 0:512:P], k.ident[0:SC, 0:SC], carried[:, 4 * q:4 * q + 4], start=False, stop=True,
                              skip_group_check=True).then_inc(s.agg_ready, 1)

                if c:
                    pe.wait_ge(s.carried_ready, N(*c) + 1)
                sum_up(0)
                sum_up(1)
                turn(0)
                if b:
                    pe.wait_ge(s.score_ready, nb + 4)
                    pe.transpose(st, score[rb][:], k.ident[:]).then_inc(s.scores_turned, 1)
                turn(1)
                if b:
                    pe.wait_ge(s.run_ready, nb + 1)
                    alone(pe, k)
                    pe.transpose(top_row, run[:, P - 1:P], k.ident[0:G, 0:G]).then_inc(s.top_turned, 1)
                turn(2)
                if b:
                    pe.wait_ge(s.cin_row_ready, nb + 1)
                    alone(pe, k)
                    pe.matmul(cin_ps, cin_row[:], k.one[0:1, 0:1], start=True, stop=True, skip_group_check=True)\
                        .then_inc(s.cin_turned, 1)
                turn(3)
                turn(4)
                sum_up(2)
                if b:
                    pe.wait_ge(s.weights_done, nb + 1)
                    pe.wait_ge(s.b_step, nb * 12 + 10)
                    alone(pe, k)
                    pe.transpose(wt_ps, wt[:, 0:P], k.ident[0:G, 0:G])
                    pe.transpose(sh_ps, shift_out[:], k.ident[0:G, 0:G]).then_inc(s.weights_turned, 1)
                add_up(0)
                turn(5)
                if b:
                    pe.wait_ge(s.scale_ready, nb + 1)
                    pe.matmul(res_ps, k.sum_rows[:], scale_d[:], start=True, stop=True, skip_group_check=True)
                add_up(1)
                add_up(2)
                sum_up(3)
                if not a:
                    sum_up(4)
                if b:
                    pe.wait_ge(s.weighted, nb + 1 + 3)
                    for j in range(G):
                        mm = pe.matmul(tail_ps[:, j:j + 1], sw[rb][:, j, :],
                                       in_last[rb][:, j:j + 1], start=True, stop=True, skip_group_check=True)
                    mm.then_inc(s.tails_ready, 1)
                if a:
                    sum_up(4)
                sum_up(5)
            in_steps(pe, step)


def build(nc, d):
    with ExitStack() as c:
        k, s = Named(), Named()

        def sb(name, shape, dt=F32):
            return c.enter_context(nc.sbuf_tensor(name, shape, dt))

        def sem(name):
            return c.enter_context(nc.semaphore(name))
        k.src_i, k.base_i = sb("src_i", [P, T], I32), sb("base_i", [1, T], I32)
        k.x, k.h, k.xlr = sb("x", [P, NT, C]), sb("h", [P, NT, C]), sb("xlr", [P, NT, 2 * C])
        k.partial = sb("partial", [SC, G + 1])
        k.hT, k.acc = sb("hT", [C + 1, NPAD]), sb("acc", [P, ACCW])
        k.ident, k.iota, k.ones = sb("ident", [P, P]), sb("iota", [P, P]), sb("ones", [P, P])
        k.iota_b = sb("iota_b", [P, LO], BF16)
        k.loc, k.in_last, k.single = sb("loc", [P, T]), sb("in_last", [P, T]), sb("single", [SC, T])
        k.cont_b, k.carry_b = sb("cont_b", [1, T]), sb("carry_b", [1, T])
        k.loop_score, k.biast, k.bias_c = sb("loop_score", [P, NT]), sb("biast", [C, LAYERS]), sb("bias_c", [C, 1])
        k.carry, k.one, k.eq = sb("carry", [1, 1]), sb("one", [1, 1]), sb("eq", [G, P + 1])
        k.sum_rows = sb("sum_rows", [G, SC])
        k.wlr_all, k.bd_all = sb("wlr_all", [C + 1, LAYERS, 2 * C]), sb("bd_all", [P, LAYERS, QUARTERS * C])
        k.att_all, k.bias_all, k.loop_all = (sb(n, [P, LAYERS, C]) for n in ("att_all", "bias_all", "loop_all"))
        k.wlr, k.bd = sb("wlr", [C + 1, 2 * C]), sb("bd", [P, QUARTERS * C])
        k.att, k.bias, k.loop = sb("att", [P, C]), sb("bias", [P, C]), sb("loop", [P, C])
        k.start_n, k.count_n = sb("start_n", [P, NT]), sb("count_n", [P, NT])
        k.wc = sb("wc", [EC, LAYERS * C])
        k.passed = sem("passed")
        with ExitStack() as early:
            def sb1(name, shape, dt=F32):
                return early.enter_context(nc.sbuf_tensor(name, shape, dt))
            k.w1, k.w2, k.b2, k.u = sb1("w1", [3 * EC + 2, HID]), sb1("w2", [HID, C]), sb1("b2", [P, C]), sb1("u", [P, 1])
            k.sq, k.spread = sb1("sq", [P, NT, C]), sb1("spread", [QUARTERS, P])
            with ExitStack() as sorting:
                def sb2(name, shape, dt=F32):
                    return sorting.enter_context(nc.sbuf_tensor(name, shape, dt))
                k.hi, k.lo = sb2("hi", [P, T], BF16), sb2("lo", [P, T], BF16)
                k.earlier, k.upper = sb2("earlier", [P, P]), sb2("upper", [HI, HI])
                k.count_ring = [sb2(f"count_ring{u}", [HI, G, LO]) for u in range(2)]
                setup(nc, k, d)
                histogram(nc, k, d)
                sort(nc, k, d)
            scan(nc, k, d)
            nodes(nc, k, d)
        s.weights_ready, s.projected, s.rows_ready_a, s.rows_ready_v = sem("weights_ready"), sem("projected"), sem("rows_ready_a"), sem("rows_ready_v")
        s.xl_out, s.sums_turned, s.sums_copied, s.h_ready = sem("xl_out"), sem("sums_turned"), sem("sums_copied"), sem("h_ready")
        s.h_turned, s.h_copied, s.pair_ready, s.pair_exp = sem("h_turned"), sem("h_copied"), sem("pair_ready"), sem("pair_exp")
        s.finish_step, s.m_ready, s.m_turned, s.m_evacuated = sem("finish_step"), sem("m_ready"), sem("m_turned"), sem("m_evacuated")
        s.e_ready, s.e_used, s.e_step, s.score_ready = sem("e_ready"), sem("e_used"), sem("e_step"), sem("score_ready")
        s.scores_turned, s.run_ready, s.top_turned, s.cin_row_ready = sem("scores_turned"), sem("run_ready"), sem("top_turned"), sem("cin_row_ready")
        s.cin_turned, s.dif_ready, s.weights_done, s.weights_turned = sem("cin_turned"), sem("dif_ready"), sem("weights_done"), sem("weights_turned")
        s.scale_ready, s.weighted, s.b_step = sem("scale_ready"), sem("weighted"), sem("b_step")
        s.agg_ready, s.agg_evacuated, s.window_done = sem("agg_ready"), sem("agg_evacuated"), sem("window_done")
        s.xr_out = sem("xr_out")
        s.loop_step, s.sums_copied_a = sem("loop_step"), sem("sums_copied_a")
        s.h_copied_v = sem("h_copied_v")
        s.tails_ready, s.carried_ready, s.c_step, s.first_id = sem("tails_ready"), sem("carried_ready"), sem("c_step"), sem("first_id")
        s.at_in, s.xw_in, s.gathered, s.ids_in, s.idx_in = (
            [sem(f"{n}{r}") for r in range(3)] for n in ("at_in", "xw_in", "gathered", "ids_in", "idx_in"))
        with nc.Block() as block:
            @block.sync
            def _(sp):
                sp.sem_inc(s.m_evacuated, 2)
                sp.sem_inc(s.e_used, 2)
                sp.sem_inc(s.e_ready, 9)
                sp.sem_inc(s.weighted, 3)
                sp.sem_inc(s.score_ready, 3)
                sp.sem_inc(s.agg_evacuated, 2)
                sp.sem_inc(s.agg_ready, 14)
                sp.sem_inc(s.window_done, 1)
        with nc.Fori(0, LAYERS) as l:
            edges(nc, k, d, s, l)
            finish(nc, k, d, s, l)
        k.sq = c.enter_context(nc.sbuf_tensor("sq_o", [P, NT, C], F32))
        output(nc, k, d)


def kernel(**inputs):
    import numpy as np
    import concourse.bacc as bacc
    from concourse.bass_utils import run_bass_kernel_spmd

    nc = bacc.Bacc("TRN2", target_bir_lowering=False, num_devices=1)
    a = {n: np.asarray(v) for n, v in inputs.items()}
    pad = ROWS - EDGES

    def tiles(v):
        return np.ascontiguousarray(np.pad(v, (0, pad), constant_values=NODES).reshape(T, P).T)
    attr = np.pad(a["edge_attr_32"], ((0, pad), (0, 0))).reshape(T, P, EC)
    dst = np.pad(a["dst"], (0, pad), constant_values=NODES)
    arrays = dict(
        src=tiles(a["src"]), dst=tiles(a["dst"]),
        dstg=dst.reshape(NG, G, P).transpose(1, 0, 2).reshape(G, NG * P),
        attr=attr.transpose(1, 0, 2),
        attrt=attr.reshape(T // 4, 4, P, EC).transpose(1, 3, 0, 2).reshape(P, T // 4 * P),
        x=np.pad(a["x"], ((0, NPAD - NODES), (0, 0))).reshape(NT, P, C).transpose(1, 0, 2),
        w1=a["L0_gnn_W1"], b1=a["L0_gnn_b1"], w2=a["L0_gnn_W2"], b2=a["L0_gnn_b2"], u=a["L0_gnn_u"],
        wembt=a["L1_gnn_W_emb"].T, bemb=a["L1_gnn_b_emb"].reshape(C, 1), wl=a["L1_gnn_Wl"], bl=a["L1_gnn_bl"],
        wr=a["L1_gnn_Wr"], br=a["L1_gnn_br"], we=a["L1_gnn_We"], att=a["L1_gnn_att"], bias=a["L1_gnn_bias"],
        biast=a["L1_gnn_bias"].T)
    arrays = {n: np.ascontiguousarray(v) for n, v in arrays.items()}
    def given(name):
        v = arrays[name]
        return nc.dram_tensor(f"in_{name}", v.shape, mybir.dt.from_np(v.dtype), kind="ExternalInput").ap()
    d = Named()
    d.src, d.dst, d.dstg, d.attr = given("src"), given("dst"), given("dstg"), given("attr")
    d.attrt, d.x, d.w1, d.b1 = given("attrt"), given("x"), given("w1"), given("b1")
    d.w2, d.b2, d.u, d.wembt = given("w2"), given("b2"), given("u"), given("wembt")
    d.bemb, d.wl, d.bl, d.wr = given("bemb"), given("wl"), given("bl"), given("wr")
    d.br, d.we, d.att, d.bias = given("br"), given("we"), given("att"), given("bias")
    d.biast = given("biast")
    d.out = nc.dram_tensor("out", (NODES, C), F32, kind="ExternalOutput").ap()
    d.tables = nc.dram_tensor("tables", (2, NPAD), F32).ap()
    d.sorted = nc.dram_tensor("sorted", (ROWS, RW), F32).ap()
    d.runs = nc.dram_tensor("runs", (ROWS, 2 * EC), F32).ap()
    d.xl_d, d.xr_d = nc.dram_tensor("xl_d", (NPAD, C), F32).ap(), nc.dram_tensor("xr_d", (NPAD + P, C), F32).ap()
    build(nc, d)
    r = run_bass_kernel_spmd(nc, [{f"in_{n}": v for n, v in arrays.items()}], core_ids=[0])
    return r.results[0]["out"]
```
